# Optimizing a Trainium2 kernel written in Bass

```python
import numpy as np
import jax
import jax.numpy as jnp

def _softmax(x, axis=-1):
    return jax.nn.softmax(x, axis=axis)

def _gelu(x):
    return jax.nn.gelu(x, approximate=True)

def _silu(x):
    return jax.nn.silu(x)

def _sigmoid(x):
    return jax.nn.sigmoid(x)

def _layernorm(x, axis=-1, eps=1e-05):
    m = jnp.mean(x, axis=axis, keepdims=True)
    v = jnp.var(x, axis=axis, keepdims=True)
    return (x - m) / jnp.sqrt(v + eps)

def _scatter_add(tgt, idx, src, axis=0):
    return tgt.at[idx].add(src)

def _segment_sum(src, seg, n):
    return jax.ops.segment_sum(src, seg, n)
kernel_name = 'mk_seq_preln_d1_jaxref_r4_acc514'

def setup_inputs(seed: int=0):
    np.random.seed(seed)
    _w = jnp.asarray

    def _L0_attn_setup():
        import jax, jax.numpy as jnp
        import numpy as np
        B, T, C = (8, 512, 256)
        NEG_INF = -1e+38

        def wkv(w, u, k, v):
            kt = jnp.swapaxes(k, 0, 1)
            vt = jnp.swapaxes(v, 0, 1)
            Bn, Cn = (k.shape[0], k.shape[2])
            aa = jnp.zeros((Bn, Cn), k.dtype)
            bb = jnp.zeros((Bn, Cn), k.dtype)
            pp = jnp.full((Bn, Cn), NEG_INF, k.dtype)

            def step(carry, kv):
                aa, bb, pp = carry
                kk, vv = kv
                ww = u + kk
                p = jnp.maximum(pp, ww)
                e1 = jnp.exp(pp - p)
                e2 = jnp.exp(ww - p)
                y = (e1 * aa + e2 * vv) / (e1 * bb + e2)
                ww2 = pp + w
                p2 = jnp.maximum(ww2, kk)
                e1 = jnp.exp(ww2 - p2)
                e2 = jnp.exp(kk - p2)
                return ((e1 * aa + e2 * vv, e1 * bb + e2, p2), y)
            _, y = jax.lax.scan(step, (aa, bb, pp), (kt, vt))
            return jnp.swapaxes(y, 0, 1)
        key = jax.random.key(seed)
        ks = jax.random.split(key, 10)
        s = 1.0 / np.sqrt(C)
        return {'x': jax.random.normal(ks[0], (B, T, C), jnp.float32), 'time_decay': jax.random.normal(ks[1], (C,), jnp.float32), 'time_first': jax.random.normal(ks[2], (C,), jnp.float32), 'time_mix_k': jax.random.uniform(ks[3], (1, 1, C), jnp.float32), 'time_mix_v': jax.random.uniform(ks[4], (1, 1, C), jnp.float32), 'time_mix_r': jax.random.uniform(ks[5], (1, 1, C), jnp.float32), 'Wk': jax.random.normal(ks[6], (C, C), jnp.float32) * s, 'Wv': jax.random.normal(ks[7], (C, C), jnp.float32) * s, 'Wr': jax.random.normal(ks[8], (C, C), jnp.float32) * s, 'Wo': jax.random.normal(ks[9], (C, C), jnp.float32) * s}
    _L0_attn_in = _L0_attn_setup()

    def _L0_ffn_setup():
        import jax, jax.numpy as jnp
        import numpy as np
        from jax import lax
        B, L, D = (4, 512, 256)
        E, TOPK = (8, 2)
        K, DIL = (3, 1)
        HID = D // 4
        EPS = 1e-06

        def _rmsnorm(h, w):
            rms = jnp.sqrt(jnp.mean(h * h, axis=-1, keepdims=True) + EPS)
            return w * (h / rms)

        def _forward(x, dw_kernel, dw_bias, pw_w, pw_b, router_w, router_b, expert_w, expert_b, out_w, out_b, norm_w, ff_down_w, ff_down_b, ff_up_w, ff_up_b):
            pad = (K - 1) * DIL
            xc = jnp.transpose(x, (0, 2, 1))
            xc = lax.conv_general_dilated(xc, dw_kernel, window_strides=(1,), padding=((pad, 0),), rhs_dilation=(DIL,), dimension_numbers=('NCH', 'OIH', 'NCH'), feature_group_count=D) + dw_bias[None, :, None]
            xc = jax.nn.silu(jnp.einsum('bdl,ed->bel', xc, pw_w) + pw_b[None, :, None])
            x1 = x + jnp.transpose(xc, (0, 2, 1))
            logits = jnp.einsum('bsd,ed->bse', x1, router_w) + router_b
            top_v, top_i = lax.top_k(logits, TOPK)
            top_w = jax.nn.softmax(top_v, axis=-1)
            rw = jnp.sum(jax.nn.one_hot(top_i, E, dtype=x1.dtype) * top_w[..., None], axis=-2)
            ye = jax.nn.silu(jnp.einsum('bsd,eod->bseo', x1, expert_w) + expert_b)
            combined = jnp.einsum('bse,bseo->bso', rw, ye)
            moe_out = jnp.einsum('bsd,od->bso', combined, out_w) + out_b
            h = _rmsnorm(x1 + moe_out, norm_w)
            ff = jax.nn.gelu(jnp.einsum('bsd,hd->bsh', h, ff_down_w) + ff_down_b, approximate=False)
            ff = jnp.einsum('bsh,dh->bsd', ff, ff_up_w) + ff_up_b
            return h + ff
        key = jax.random.key(seed)
        ks = jax.random.split(key, 16)
        s = 0.02
        return {'x': jax.random.normal(ks[0], (B, L, D), dtype=jnp.float32), 'dw_kernel': jax.random.normal(ks[1], (D, 1, K), dtype=jnp.float32) * s, 'dw_bias': jnp.zeros((D,), dtype=jnp.float32), 'pw_w': jax.random.normal(ks[2], (D, D), dtype=jnp.float32) * s, 'pw_b': jnp.zeros((D,), dtype=jnp.float32), 'router_w': jax.random.normal(ks[3], (E, D), dtype=jnp.float32) * s, 'router_b': jnp.zeros((E,), dtype=jnp.float32), 'expert_w': jax.random.normal(ks[4], (E, D, D), dtype=jnp.float32) * s, 'expert_b': jnp.zeros((E, D), dtype=jnp.float32), 'out_w': jax.random.normal(ks[5], (D, D), dtype=jnp.float32) * s, 'out_b': jnp.zeros((D,), dtype=jnp.float32), 'norm_w': jnp.ones((D,), dtype=jnp.float32), 'ff_down_w': jax.random.normal(ks[6], (HID, D), dtype=jnp.float32) * s, 'ff_down_b': jnp.zeros((HID,), dtype=jnp.float32), 'ff_up_w': jax.random.normal(ks[7], (D, HID), dtype=jnp.float32) * s, 'ff_up_b': jnp.zeros((D,), dtype=jnp.float32)}
    _L0_ffn_in = _L0_ffn_setup()
    _d = {'L0_attn_x': _L0_attn_in['x'], 'L0_attn_time_decay': _L0_attn_in['time_decay'], 'L0_attn_time_first': _L0_attn_in['time_first'], 'L0_attn_time_mix_k': _L0_attn_in['time_mix_k'], 'L0_attn_time_mix_v': _L0_attn_in['time_mix_v'], 'L0_attn_time_mix_r': _L0_attn_in['time_mix_r'], 'L0_attn_Wk': _L0_attn_in['Wk'], 'L0_attn_Wv': _L0_attn_in['Wv'], 'L0_attn_Wr': _L0_attn_in['Wr'], 'L0_attn_Wo': _L0_attn_in['Wo'], 'L0_ffn_dw_kernel': _L0_ffn_in['dw_kernel'], 'L0_ffn_dw_bias': _L0_ffn_in['dw_bias'], 'L0_ffn_pw_w': _L0_ffn_in['pw_w'], 'L0_ffn_pw_b': _L0_ffn_in['pw_b'], 'L0_ffn_router_w': _L0_ffn_in['router_w'], 'L0_ffn_router_b': _L0_ffn_in['router_b'], 'L0_ffn_expert_w': _L0_ffn_in['expert_w'], 'L0_ffn_expert_b': _L0_ffn_in['expert_b'], 'L0_ffn_out_w': _L0_ffn_in['out_w'], 'L0_ffn_out_b': _L0_ffn_in['out_b'], 'L0_ffn_norm_w': _L0_ffn_in['norm_w'], 'L0_ffn_ff_down_w': _L0_ffn_in['ff_down_w'], 'L0_ffn_ff_down_b': _L0_ffn_in['ff_down_b'], 'L0_ffn_ff_up_w': _L0_ffn_in['ff_up_w'], 'L0_ffn_ff_up_b': _L0_ffn_in['ff_up_b']}
    _x0 = _d['L0_attn_x']
    _d['L0_attn_x'] = jax.random.normal(jax.random.fold_in(jax.random.key(seed), 1), (16, 512, 256), dtype=_x0.dtype)
    del _x0
    return _d

def reference(L0_attn_x, L0_attn_time_decay, L0_attn_time_first, L0_attn_time_mix_k, L0_attn_time_mix_v, L0_attn_time_mix_r, L0_attn_Wk, L0_attn_Wv, L0_attn_Wr, L0_attn_Wo, L0_ffn_dw_kernel, L0_ffn_dw_bias, L0_ffn_pw_w, L0_ffn_pw_b, L0_ffn_router_w, L0_ffn_router_b, L0_ffn_expert_w, L0_ffn_expert_b, L0_ffn_out_w, L0_ffn_out_b, L0_ffn_norm_w, L0_ffn_ff_down_w, L0_ffn_ff_down_b, L0_ffn_ff_up_w, L0_ffn_ff_up_b):

    def _L0_attn_ref(x, time_decay, time_first, time_mix_k, time_mix_v, time_mix_r, Wk, Wv, Wr, Wo):
        import jax, jax.numpy as jnp
        import numpy as np
        B, T, C = (8, 512, 256)
        NEG_INF = -1e+38

        def wkv(w, u, k, v):
            kt = jnp.swapaxes(k, 0, 1)
            vt = jnp.swapaxes(v, 0, 1)
            Bn, Cn = (k.shape[0], k.shape[2])
            aa = jnp.zeros((Bn, Cn), k.dtype)
            bb = jnp.zeros((Bn, Cn), k.dtype)
            pp = jnp.full((Bn, Cn), NEG_INF, k.dtype)

            def step(carry, kv):
                aa, bb, pp = carry
                kk, vv = kv
                ww = u + kk
                p = jnp.maximum(pp, ww)
                e1 = jnp.exp(pp - p)
                e2 = jnp.exp(ww - p)
                y = (e1 * aa + e2 * vv) / (e1 * bb + e2)
                ww2 = pp + w
                p2 = jnp.maximum(ww2, kk)
                e1 = jnp.exp(ww2 - p2)
                e2 = jnp.exp(kk - p2)
                return ((e1 * aa + e2 * vv, e1 * bb + e2, p2), y)
            _, y = jax.lax.scan(step, (aa, bb, pp), (kt, vt))
            return jnp.swapaxes(y, 0, 1)
        xx = jnp.pad(x, ((0, 0), (1, 0), (0, 0)))[:, :-1, :]
        xk = x * time_mix_k + xx * (1.0 - time_mix_k)
        xv = x * time_mix_v + xx * (1.0 - time_mix_v)
        xr = x * time_mix_r + xx * (1.0 - time_mix_r)
        k = jnp.einsum('btc,dc->btd', xk, Wk)
        v = jnp.einsum('btc,dc->btd', xv, Wv)
        r = jnp.einsum('btc,dc->btd', xr, Wr)
        w = -jnp.exp(time_decay)
        rwkv = jax.nn.sigmoid(r) * wkv(w, time_first, k, v)
        return jnp.einsum('btc,dc->btd', rwkv, Wo)

    def _L0_ffn_ref(x, dw_kernel, dw_bias, pw_w, pw_b, router_w, router_b, expert_w, expert_b, out_w, out_b, norm_w, ff_down_w, ff_down_b, ff_up_w, ff_up_b):
        import jax, jax.numpy as jnp
        import numpy as np
        from jax import lax
        B, L, D = (4, 512, 256)
        E, TOPK = (8, 2)
        K, DIL = (3, 1)
        HID = D // 4
        EPS = 1e-06

        def _rmsnorm(h, w):
            rms = jnp.sqrt(jnp.mean(h * h, axis=-1, keepdims=True) + EPS)
            return w * (h / rms)

        def _forward(x, dw_kernel, dw_bias, pw_w, pw_b, router_w, router_b, expert_w, expert_b, out_w, out_b, norm_w, ff_down_w, ff_down_b, ff_up_w, ff_up_b):
            pad = (K - 1) * DIL
            xc = jnp.transpose(x, (0, 2, 1))
            xc = lax.conv_general_dilated(xc, dw_kernel, window_strides=(1,), padding=((pad, 0),), rhs_dilation=(DIL,), dimension_numbers=('NCH', 'OIH', 'NCH'), feature_group_count=D) + dw_bias[None, :, None]
            xc = jax.nn.silu(jnp.einsum('bdl,ed->bel', xc, pw_w) + pw_b[None, :, None])
            x1 = x + jnp.transpose(xc, (0, 2, 1))
            logits = jnp.einsum('bsd,ed->bse', x1, router_w) + router_b
            top_v, top_i = lax.top_k(logits, TOPK)
            top_w = jax.nn.softmax(top_v, axis=-1)
            rw = jnp.sum(jax.nn.one_hot(top_i, E, dtype=x1.dtype) * top_w[..., None], axis=-2)
            ye = jax.nn.silu(jnp.einsum('bsd,eod->bseo', x1, expert_w) + expert_b)
            combined = jnp.einsum('bse,bseo->bso', rw, ye)
            moe_out = jnp.einsum('bsd,od->bso', combined, out_w) + out_b
            h = _rmsnorm(x1 + moe_out, norm_w)
            ff = jax.nn.gelu(jnp.einsum('bsd,hd->bsh', h, ff_down_w) + ff_down_b, approximate=False)
            ff = jnp.einsum('bsh,dh->bsd', ff, ff_up_w) + ff_up_b
            return h + ff
        return _forward(x, dw_kernel, dw_bias, pw_w, pw_b, router_w, router_b, expert_w, expert_b, out_w, out_b, norm_w, ff_down_w, ff_down_b, ff_up_w, ff_up_b)
    x = L0_attn_x
    x = x + _L0_attn_ref(_layernorm(x, axis=-1), L0_attn_time_decay, L0_attn_time_first, L0_attn_time_mix_k, L0_attn_time_mix_v, L0_attn_time_mix_r, L0_attn_Wk, L0_attn_Wv, L0_attn_Wr, L0_attn_Wo)
    x = x + _L0_ffn_ref(_layernorm(x, axis=-1), L0_ffn_dw_kernel, L0_ffn_dw_bias, L0_ffn_pw_w, L0_ffn_pw_b, L0_ffn_router_w, L0_ffn_router_b, L0_ffn_expert_w, L0_ffn_expert_b, L0_ffn_out_w, L0_ffn_out_b, L0_ffn_norm_w, L0_ffn_ff_down_w, L0_ffn_ff_down_b, L0_ffn_ff_up_w, L0_ffn_ff_up_b)
    return x

_drawn_inputs = setup_inputs


def setup_inputs(seed=0):
    import zlib

    import numpy as np

    out = dict(_drawn_inputs(seed))
    spreads = {'L0_ffn_dw_bias': (0.0, 0.8),
     'L0_ffn_pw_b': (0.0, 0.289),
     'L0_ffn_router_b': (0.0, 0.8),
     'L0_ffn_expert_b': (0.0, 0.8),
     'L0_ffn_out_b': (0.0, 0.1),
     'L0_ffn_norm_w': (1.0, 0.2),
     'L0_ffn_ff_down_b': (0.0, 0.8),
     'L0_ffn_ff_up_b': (0.0, 0.1)}
    factors = {'L0_ffn_dw_kernel': 8.0,
     'L0_ffn_pw_w': 7.119,
     'L0_ffn_router_w': 3.415,
     'L0_ffn_expert_w': 3.023,
     'L0_ffn_out_w': 2.823,
     'L0_ffn_ff_down_w': 4.098,
     'L0_ffn_ff_up_w': 3.812}
    for name, (base, spread) in spreads.items():
        noise = np.random.default_rng([zlib.crc32(name.encode()), seed]).standard_normal(out[name].shape)
        drawn = base * np.exp(spread * noise) if base else spread * noise
        out[name] = jnp.asarray(drawn.astype(out[name].dtype))
    for name, factor in factors.items():
        out[name] = (out[name] * factor).astype(out[name].dtype)
    return out
```

```python
from contextlib import ExitStack

import concourse.bass as bass
from concourse import mybir

F32 = mybir.dt.float32
F16 = mybir.dt.float16
AX_X = mybir.AxisListType.X
ALU = mybir.AluOpType
ACT = mybir.ActivationFunctionType

P = 128
NEG_INF = -1e38
LN_EPS = 1e-5
RMS_EPS = 1e-6
WSCALE = 64.0

VECS = ["time_decay", "time_first", "mix_k", "mix_v", "mix_r", "conv0", "conv1", "conv2", "conv_b", "pw_b"]


class Signal:

    def __init__(self, sem, per):
        self.sem, self.per = sem, per

    def at(self, seq, n=None):
        return self.per * seq + (self.per if n is None else n)

    def rises(self, seq, n):
        value = self.at(seq, n)
        return not isinstance(value, int) or value > 0


def past(seq, back=1):
    return not isinstance(seq, int) or seq >= back


def build(nc, x, vecs, w_attn, w_pw, w_router, w_expert, w_out, w_down, w_up, b_rows, b_down, norm_w, out):
    B, T, C = x.shape
    H = C // P
    NT = T // P
    NE = w_router.shape[1]
    HID = w_down.shape[1]
    NG = NE * C // T
    EPG = NE // NG
    RB, OB, UB = NE * C, NE * C + NE, NE * C + NE + C
    NROW = UB + C
    NV = len(VECS)

    with ExitStack() as ctx:
        def sb(name, shape, dt=F32):
            return ctx.enter_context(nc.sbuf_tensor(name, shape, dt))

        def ps(name, shape):
            return ctx.enter_context(nc.psum_tensor(name, shape, F32))

        def sig(name, per):
            return Signal(ctx.enter_context(nc.semaphore(name)), per)

        vec = sb("vec", [P, NV, H])
        decay = sb("decay", [P, H])
        neg_first = sb("neg_first", [P, H])
        wa = sb("wa", [P, 4, H, C])
        wpw = sb("wpw", [P, H, C])
        wo2 = sb("wo2", [P, H, C])
        wout = sb("wout", [P, H, C])
        wdown = sb("wdown", [P, H, HID])
        wup = sb("wup", [HID, C])
        bdown = sb("bdown", [HID, 1])
        wrout = sb("wrout", [P, H, NE])
        wrh = sb("wrh", [P, H, NE], F16)
        wrl = sb("wrl", [P, H, NE], F16)
        weh = sb("weh", [P, H, NE * C], F16)
        wel = sb("wel", [P, H, NE * C], F16)
        rows = sb("rows", [2, NROW])
        rows_l = sb("rows_l", [2, NROW], F16)
        brow = sb("brow", [2, NROW], F16)
        row_is = sb("row_is", [2, 2])
        ones2 = sb("ones2", [2, P], F16)
        one = sb("one", [P, 1])
        normw = sb("normw", [P, C])
        ident = sb("ident", [P, P])
        ident16 = sb("ident16", [P, P], F16)
        rank = sb("rank", [P, NT, NE])
        minus_half = sb("minus_half", [P, NT])
        sqrt_c = sb("sqrt_c", [P, NT])
        rms_eps_c = sb("rms_eps_c", [P, NT])

        xa = sb("xa", [P, NT, C])
        st1 = sb("st1", [P, NT, 6])
        mo1 = sb("mo1", [P, 4, NT])
        pw1 = sb("pw1", [P, NT])
        rstd1 = sb("rstd1", [P, NT])
        xn1 = sb("xn1", [P, NT, C])
        xt1 = sb("xt1", [P, H, 1 + T])
        xd = sb("xd", [P, H, T])
        xk = sb("xk", [P, H, T])
        xv = sb("xv", [P, H, T])
        xr = sb("xr", [P, H, T])
        kk = sb("kk", [P, H, T])
        vv = sb("vv", [P, H, T])
        pp = sb("pp", [P, H, 1 + T])
        fd = sb("fd", [P, H, T])
        gd = sb("gd", [P, H, T])
        sd = sb("sd", [P, H, T])
        ev = sb("ev", [P, H, T])
        aa = sb("aa", [P, H, 1 + T])
        bb = sb("bb", [P, H, 1 + T])
        num = sb("num", [P, H, T])
        den = sb("den", [P, H, T])
        tr = sb("tr", [P, H, T])
        rwkv = sb("rwkv", [P, H, T])
        xres = sb("xres", [P, NT, C])
        x2 = sb("x2", [P, NT, C])
        st2 = sb("st2", [P, NT, 6])
        mo2 = sb("mo2", [P, 4, NT])
        pw2 = sb("pw2", [P, NT])
        rstd2 = sb("rstd2", [P, NT])
        xn2 = sb("xn2", [P, NT, C])
        xt2 = sb("xt2", [P, H, 2 + T])
        cv = sb("cv", [P, H, T])
        s1 = sb("s1", [P, H, T])
        x1 = sb("x1", [P, H, T])
        x1h = sb("x1h", [P, H, T], F16)
        x1l = sb("x1l", [P, H, T], F16)
        lg = sb("lg", [P, NT, NE])
        lg2 = sb("lg2", [P, NT, NE])
        hit = sb("hit", [P, 2, NT, NE])
        top = sb("top", [P, 2, NT])
        first = sb("first", [P, 2, NT])
        gap = sb("gap", [P, NT])
        th = sb("th", [P, NT])
        w12 = sb("w12", [P, 2, NT])
        sel = sb("sel", [P, 2, NT, NE])
        rw = sb("rw", [P, NT, NE])
        NY = 4
        ye = sb("ye", [P, NY, T])
        wstage = ye[:].rearrange("p y t -> p (y t)")
        comb = sb("comb", [P, NT, C])
        combt = sb("combt", [P, H, T])
        sq = sb("sq", [P, C])
        ms = sb("ms", [P, NT])
        msv = sb("msv", [P, NT])
        msp = sb("msp", [P, NT])
        rms = sb("rms", [P, NT])
        hh = sb("hh", [P, NT, C])
        ht = sb("ht", [P, H, T])
        xh = sb("xh", [P, NT, C])
        ffg = sb("ffg", [HID, T])
        yo = sb("yo", [P, NT, C])

        pt = ps("pt", [P, 2, T])
        pk = ps("pk", [P, 2, T])
        pe = ps("pe", [P, 2, T])
        po = ps("po", [P, 2, 2, C])

        vecs_in = sig("vecs_in", 16)
        attn_w_in = sig("attn_w_in", 16)
        small_w_in = sig("small_w_in", 16 * 9)
        stage_in = sig("stage_in", 16)
        decay_exp = sig("decay_exp", 1)
        pool_const = sig("pool_const", 5)
        dve_const = sig("dve_const", 1)
        x_in = sig("x_in", 16)
        stats1 = sig("stats1", NT)
        moments1 = sig("moments1", 6)
        rstd1_ready = sig("rstd1_ready", 2)
        xn1_ready = sig("xn1_ready", NT)
        t1_done = sig("t1_done", 2)
        xt1_ready = sig("xt1_ready", 2)
        mixed = sig("mixed", 7)
        kvr_done = sig("kvr_done", 6)
        k_ready = sig("k_ready", 2)
        v_ready = sig("v_ready", 2)
        tr_ready = sig("tr_ready", 2)
        p_ready = sig("p_ready", 2)
        diffs = sig("diffs", 3)
        e1_ready = sig("e1_ready", 2)
        e2_ready = sig("e2_ready", 1)
        sg_ready = sig("sg_ready", 2)
        wkv = sig("wkv", 11)
        ln_ready = sig("ln_ready", 1)
        rec_ready = sig("rec_ready", 1)
        wo_done = sig("wo_done", 2)
        xres_in = sig("xres_in", 16)
        x2_ready = sig("x2_ready", 2)
        stats2 = sig("stats2", NT)
        moments2 = sig("moments2", 6)
        rstd2_ready = sig("rstd2_ready", 2)
        xn2_ready = sig("xn2_ready", NT)
        t2_done = sig("t2_done", 2)
        xt2_ready = sig("xt2_ready", 2)
        tap_ready = sig("tap_ready", 2)
        conv = sig("conv", 4)
        pw_done = sig("pw_done", 2)
        s1_ready = sig("s1_ready", 2)
        x1_ready = sig("x1_ready", 2)
        x1h_ready = sig("x1h_ready", 2)
        x1l_ready = sig("x1l_ready", 2)
        routed = sig("routed", 1)
        logits_read = sig("logits_read", 1)
        picks = sig("picks", 11)
        route = sig("route", 5)
        tanh_ready = sig("tanh_ready", 1)
        expert_done = sig("expert_done", NT * NG)
        ye_ready = sig("ye_ready", NT * NG)
        combined = sig("combined", NT * NE)
        t3_done = sig("t3_done", NT)
        combt_ready = sig("combt_ready", NT)
        moe_done = sig("moe_done", 2)
        ms_ready = sig("ms_ready", NT)
        rms_ready = sig("rms_ready", 6)
        h_ready = sig("h_ready", NT)
        xh_ready = sig("xh_ready", 2)
        t4_done = sig("t4_done", 2)
        ht_ready = sig("ht_ready", 2)
        down_done = sig("down_done", 1)
        ffg_ready = sig("ffg_ready", 1)
        up_done = sig("up_done", 2)
        y_ready = sig("y_ready", 2)
        stored = sig("stored", 16)

        x_tok = x.rearrange("b (t p) c -> b p t c", p=P)
        out_tok = out.rearrange("b (t p) c -> b p t c", p=P)
        DVE_CONST = 19 + 2 * H

        def dram_seq(ap, seq):
            return ap[bass.ds(seq, 1)].rearrange("a p t c -> p (a t) c")

        def schedule(eng, body):
            body(None, None, 0)
            body(None, 0, 1)
            body(0, 1, 2)
            with eng.Fori(1, B - 2) as f:
                body(f, f + 1, f + 2)
            body(B - 2, B - 1, None)
            body(B - 1, None, None)

        block = ctx.enter_context(nc.Block())

        @block.sync
        def _(sp):
            def load_x(n):
                if past(n):
                    sp.wait_ge(xn1_ready.sem, xn1_ready.at(n - 1))
                sp.dma_start(xa[:], dram_seq(x_tok, n)).then_inc(x_in.sem, 16)

            def load_residual(a):
                if past(a):
                    sp.wait_ge(x2_ready.sem, x2_ready.at(a - 1))
                sp.dma_start(xres[:], dram_seq(x_tok, a)).then_inc(xres_in.sem, 16)

            load_x(0)
            sp.dma_start(vec[:], vecs).then_inc(vecs_in.sem, 16)
            sp.dma_start(wa[:], w_attn.rearrange("m (h p) c -> p m h c", p=P)).then_inc(attn_w_in.sem, 16)
            halves = lambda w: w.rearrange("(h p) c -> p h c", p=P)
            sp.dma_start(wstage, w_expert[0:P, :]).then_inc(stage_in.sem, 16)
            sp.dma_start(wpw[:], halves(w_pw)).then_inc(small_w_in.sem, 16)
            sp.dma_start(wrout[:], halves(w_router)).then_inc(small_w_in.sem, 16)
            sp.dma_start(wout[:], halves(w_out)).then_inc(small_w_in.sem, 16)
            sp.dma_start(wdown[:], halves(w_down)).then_inc(small_w_in.sem, 16)
            sp.dma_start(wup[:], w_up).then_inc(small_w_in.sem, 16)
            sp.dma_start(bdown[:], b_down).then_inc(small_w_in.sem, 16)
            sp.dma_start(normw[:], norm_w.to_broadcast([P, C])).then_inc(small_w_in.sem, 16)
            for r in range(2):
                sp.dma_start(rows[r:r + 1, :], b_rows).then_inc(small_w_in.sem, 16)
            for h in range(1, H):
                sp.wait_ge(dve_const.sem, 2 * h)
                sp.dma_start(wstage, w_expert[h * P:(h + 1) * P, :]).then_inc(stage_in.sem, 16)

            def body(f, a, n):
                if n is not None and not (isinstance(n, int) and n == 0):
                    load_x(n)
                if a is not None:
                    load_residual(a)
                if f is not None:
                    sp.wait_ge(y_ready.sem, y_ready.at(f))
                    sp.dma_start(dram_seq(out_tok, f), yo[:]).then_inc(stored.sem, 16)

            schedule(sp, body)
            sp.wait_ge(stored.sem, stored.at(B - 1))

        @block.gpsimd
        def _(pool):
            nc.gpsimd.memset(ident[:], 0.0).then_inc(pool_const.sem, 1)
            pool.wait_ge(pool_const.sem, 1)
            nc.gpsimd.affine_select(out=ident[:], in_=ident[:], compare_op=ALU.not_equal, fill=1.0, base=0,
                                    pattern=[[-1, P]], channel_multiplier=1).then_inc(pool_const.sem, 1)
            nc.gpsimd.memset(minus_half[:], -0.5).then_inc(pool_const.sem, 1)
            nc.gpsimd.memset(sqrt_c[:], float(C) ** 0.5).then_inc(pool_const.sem, 1)
            nc.gpsimd.memset(rms_eps_c[:], RMS_EPS * C).then_inc(pool_const.sem, 1)
            pool.wait_ge(pool_const.sem, 5)

            def rstd(seq, mo, pw, dst, moments, ready, used):
                pool.wait_ge(moments.sem, moments.at(seq))
                if past(seq):
                    pool.wait_ge(ready.sem, ready.at(seq - 1))
                if past(seq):
                    pool.wait_ge(used.sem, used.at(seq - 1))
                nc.gpsimd.tensor_tensor(pw[:], mo[:, 3], minus_half[:], ALU.pow).then_inc(ready.sem, 1)
                pool.wait_ge(ready.sem, ready.at(seq, 1))
                nc.gpsimd.tensor_tensor(dst[:], pw[:], sqrt_c[:], ALU.mult).then_inc(ready.sem, 1)

            def body(f, a, n):
                if f is not None:
                    for b in range(2):
                        t = slice(2 * b, 2 * b + 2)
                        pool.wait_ge(ms_ready.sem, ms_ready.at(f, 2 * b + 2))
                        if past(f):
                            pool.wait_ge(rms_ready.sem, rms_ready.at(f - 1))
                        if past(f):
                            pool.wait_ge(h_ready.sem, h_ready.at(f - 1))
                        nc.gpsimd.tensor_tensor(msv[:, t], ms[:, t], rms_eps_c[:, t], ALU.add).then_inc(rms_ready.sem, 1)
                        pool.wait_ge(rms_ready.sem, rms_ready.at(f, 3 * b + 1))
                        nc.gpsimd.tensor_tensor(msp[:, t], msv[:, t], minus_half[:, t],
                                                ALU.pow).then_inc(rms_ready.sem, 1)
                        pool.wait_ge(rms_ready.sem, rms_ready.at(f, 3 * b + 2))
                        nc.gpsimd.tensor_tensor(rms[:, t], msp[:, t], sqrt_c[:, t], ALU.mult).then_inc(rms_ready.sem, 1)
                if n is not None:
                    rstd(n, mo1, pw1, rstd1, moments1, rstd1_ready, xn1_ready)
                if a is not None:
                    rstd(a, mo2, pw2, rstd2, moments2, rstd2_ready, xn2_ready)

            schedule(pool, body)

        @block.tensor
        def _(te):
            def transpose_all(src, done, seq):
                for h in range(H):
                    for t in range(NT):
                        mm = nc.tensor.transpose(pt[:, h, t * P:(t + 1) * P], src[:, t, h * P:(h + 1) * P], ident[:])
                    mm.then_inc(done.sem, 1)

            def product(dst, weight, m, src, done):
                for h in range(H):
                    mm = nc.tensor.matmul(dst, weight[:, h, m * P:(m + 1) * P], src[:, h, :],
                                          start=h == 0, stop=h == H - 1)
                mm.then_inc(done.sem, 1)

            def body(f, a, n):
                if f is not None:
                    te.wait_ge(xn2_ready.sem, xn2_ready.at(f))
                    if past(f):
                        te.wait_ge(ht_ready.sem, ht_ready.at(f - 1))
                    if n is None:
                        te.wait_ge(xt1_ready.sem, xt1_ready.at(B - 1))
                    else:
                        if past(n):
                            te.wait_ge(xt1_ready.sem, xt1_ready.at(n - 1))
                    transpose_all(xn2, t2_done, f)
                if a is not None:
                    for g, (m, src) in enumerate(((0, xk), (1, xv))):
                        for half in range(H):
                            te.wait_ge(mixed.sem, mixed.at(a, 1 + H * (g + 1)))
                            if g == 0:
                                if half == 0:
                                    if past(a, 2):
                                        te.wait_ge(logits_read.sem, logits_read.at(a - 2))
                                else:
                                    if past(a, 2):
                                        te.wait_ge(ffg_ready.sem, ffg_ready.at(a - 2))
                                if past(a):
                                    te.wait_ge(tr_ready.sem, tr_ready.at(a - 1, half + 1))
                            else:
                                te.wait_ge(k_ready.sem, k_ready.at(a, half + 1))
                            product(pk[:, half, :], wa[:, m], half, src, kvr_done)
                if f is not None:
                    for half in range(H):
                        te.wait_ge(conv.sem, conv.at(f))
                        if a is not None:
                            te.wait_ge(v_ready.sem, v_ready.at(a, half + 1))
                        else:
                            if past(f):
                                te.wait_ge(logits_read.sem, logits_read.at(f - 1))
                            if past(f):
                                te.wait_ge(ffg_ready.sem, ffg_ready.at(f - 1))
                            te.wait_ge(tr_ready.sem, tr_ready.at(f, half + 1))
                        product(pk[:, half, :], wpw, half, cv, pw_done)
                if a is not None:
                    for half in range(H):
                        te.wait_ge(mixed.sem, mixed.at(a))
                        if f is not None:
                            te.wait_ge(s1_ready.sem, s1_ready.at(f, half + 1))
                        else:
                            te.wait_ge(v_ready.sem, v_ready.at(a, half + 1))
                        product(pk[:, half, :], wa[:, 2], half, xr, kvr_done)
                if f is not None:
                    te.wait_ge(x1h_ready.sem, x1h_ready.at(f))
                    te.wait_ge(x1l_ready.sem, x1l_ready.at(f))
                    if a is not None:
                        te.wait_ge(tr_ready.sem, tr_ready.at(a, 1))
                    else:
                        te.wait_ge(s1_ready.sem, s1_ready.at(f, 1))
                    for t in range(NT):
                        tok = slice(t * P, (t + 1) * P)
                        dst = pk[:, 0, t * NE:(t + 1) * NE]
                        nc.tensor.matmul(dst, ones2[:], brow[:, RB:RB + NE], start=True, stop=False)
                        for h in range(H):
                            nc.tensor.matmul(dst, x1h[:, h, tok], wrh[:, h, :], start=False, stop=False)
                            nc.tensor.matmul(dst, x1h[:, h, tok], wrl[:, h, :], start=False, stop=False)
                            mm = nc.tensor.matmul(dst, x1l[:, h, tok], wrh[:, h, :], start=False, stop=h == H - 1)
                    mm.then_inc(routed.sem, 1)

                    def experts(t):
                        tok = slice(t * P, (t + 1) * P)
                        for g in range(NG):
                            i = t * NG + g
                            if ye_ready.rises(f, i - 1):
                                te.wait_ge(ye_ready.sem, ye_ready.at(f, i - 1))
                            dst, cols = pe[:, i % 2, :], slice(g * T, (g + 1) * T)
                            nc.tensor.matmul(dst, ones2[:], brow[:, cols], start=True, stop=False)
                            for h in range(H):
                                nc.tensor.matmul(dst, x1h[:, h, tok], weh[:, h, cols], start=False, stop=False)
                                nc.tensor.matmul(dst, x1h[:, h, tok], wel[:, h, cols], start=False, stop=False)
                                mm = nc.tensor.matmul(dst, x1l[:, h, tok], weh[:, h, cols], start=False,
                                                      stop=h == H - 1)
                            mm.then_inc(expert_done.sem, 1)

                    def turn_combined(t):
                        te.wait_ge(combined.sem, combined.at(f, NE * (t + 1)))
                        if t < 2:
                            te.wait_ge(xt2_ready.sem, xt2_ready.at(f, t + 1))
                        else:
                            te.wait_ge(combt_ready.sem, combt_ready.at(f, t - 1))
                        for h in range(H):
                            mm = nc.tensor.transpose(pt[:, t % 2, h * P:(h + 1) * P], comb[:, t, h * P:(h + 1) * P],
                                                     ident[:])
                        mm.then_inc(t3_done.sem, 1)

                    def mix_out(b):
                        if past(f):
                            te.wait_ge(y_ready.sem, y_ready.at(f - 1))
                        if a is not None:
                            if past(a):
                                te.wait_ge(x2_ready.sem, x2_ready.at(a - 1, b + 1))
                        else:
                            te.wait_ge(x2_ready.sem, x2_ready.at(f, b + 1))
                        for t in range(2 * b, 2 * b + 2):
                            tok = slice(t * P, (t + 1) * P)
                            te.wait_ge(combt_ready.sem, combt_ready.at(f, t + 1))
                            dst = po[:, b, t % 2, :]
                            nc.tensor.matmul(dst, ones2[:], brow[:, OB:OB + C], start=True, stop=False)
                            for h in range(H):
                                part = dst[:, h * P:(h + 1) * P]
                                nc.tensor.matmul(part, x1h[:, h, tok], ident16[:], start=False, stop=False)
                                nc.tensor.matmul(part, x1l[:, h, tok], ident16[:], start=False, stop=False)
                            for h in range(H):
                                mm = nc.tensor.matmul(dst, combt[:, h, tok], wout[:, h, :], start=False,
                                                      stop=h == H - 1)
                        mm.then_inc(moe_done.sem, 1)

                    experts(0)
                    experts(1)
                    turn_combined(0)
                    experts(2)
                    turn_combined(1)
                    mix_out(0)
                    experts(3)
                    turn_combined(2)
                    turn_combined(3)
                    mix_out(1)
                    te.wait_ge(h_ready.sem, h_ready.at(f))
                    te.wait_ge(combt_ready.sem, combt_ready.at(f))
                    transpose_all(hh, t4_done, f)
                if a is not None:
                    for b in range(2):
                        te.wait_ge(wkv.sem, wkv.at(a))
                        if f is not None:
                            te.wait_ge(h_ready.sem, h_ready.at(f, 2 * b + 2))
                        for t in range(2 * b, 2 * b + 2):
                            for h in range(H):
                                mm = nc.tensor.matmul(po[:, b, t % 2, :], rwkv[:, h, t * P:(t + 1) * P], wo2[:, h, :],
                                                      start=h == 0, stop=h == H - 1)
                        mm.then_inc(wo_done.sem, 1)
                if f is not None:
                    te.wait_ge(ht_ready.sem, ht_ready.at(f))
                    if a is not None:
                        te.wait_ge(tr_ready.sem, tr_ready.at(a))
                    for h in range(H):
                        mm = nc.tensor.matmul(pk[0:HID, 1, :], wdown[:, h, :], ht[:, h, :], start=h == 0,
                                              stop=h == H - 1)
                    mm.then_inc(down_done.sem, 1)
                if n is not None:
                    te.wait_ge(xn1_ready.sem, xn1_ready.at(n))
                    if f is None:
                        if past(n):
                            te.wait_ge(xt1_ready.sem, xt1_ready.at(n - 1))
                    transpose_all(xn1, t1_done, n)
                if f is not None:
                    te.wait_ge(ffg_ready.sem, ffg_ready.at(f))
                    for b in range(2):
                        if a is not None:
                            te.wait_ge(x2_ready.sem, x2_ready.at(a, b + 1))
                        else:
                            te.wait_ge(h_ready.sem, h_ready.at(f))
                        for t in range(2 * b, 2 * b + 2):
                            dst = po[:, b, t % 2, :]
                            nc.tensor.matmul(dst, ones2[:], brow[:, UB:UB + C], start=True, stop=False)
                            mm = nc.tensor.matmul(dst, ffg[:, t * P:(t + 1) * P], wup[:], start=False, stop=True)
                        mm.then_inc(up_done.sem, 1)

            te.wait_ge(attn_w_in.sem, 16)
            te.wait_ge(small_w_in.sem, small_w_in.per)
            te.wait_ge(pool_const.sem, 5)
            te.wait_ge(dve_const.sem, DVE_CONST)
            schedule(te, body)

        @block.scalar
        def _(act):
            act.wait_ge(vecs_in.sem, 16)
            act.activation(decay[:], vec[:, 0, :], ACT.Exp).then_inc(decay_exp.sem, 1)
            act.wait_ge(small_w_in.sem, small_w_in.per)
            act.wait_ge(dve_const.sem, DVE_CONST)

            def body(f, a, n):
                if f is not None:
                    for h in range(H):
                        act.wait_ge(t2_done.sem, t2_done.at(f, h + 1))
                        if past(f):
                            act.wait_ge(x1_ready.sem, x1_ready.at(f - 1, h + 1))
                        act.copy(xt2[:, h, 2:2 + T], pt[:, h, :]).then_inc(xt2_ready.sem, 1)
                    for h in range(H):
                        act.wait_ge(xt2_ready.sem, xt2_ready.at(f, h + 1))
                        if past(f):
                            act.wait_ge(pw_done.sem, pw_done.at(f - 1))
                        act.activation(cv[:, h, :], xt2[:, h, 2:2 + T], ACT.Identity, bias=vec[:, 8, h:h + 1],
                                       scale=vec[:, 7, h:h + 1]).then_inc(tap_ready.sem, 1)
                if a is not None:
                    if past(a):
                        act.wait_ge(diffs.sem, diffs.at(a - 1))
                    for h in range(H):
                        act.wait_ge(kvr_done.sem, kvr_done.at(a, h + 1))
                        act.copy(kk[:, h, :], pk[:, h, :]).then_inc(k_ready.sem, 1)
                    if past(a):
                        act.wait_ge(wkv.sem, wkv.at(a - 1))
                    for h in range(H):
                        act.wait_ge(kvr_done.sem, kvr_done.at(a, H + h + 1))
                        act.copy(vv[:, h, :], pk[:, h, :]).then_inc(v_ready.sem, 1)
                    act.wait_ge(diffs.sem, diffs.at(a, 1))
                    for h in range(H):
                        act.activation(fd[:, h, :], fd[:, h, :], ACT.Exp, bias=decay[:, h:h + 1]).then_inc(e1_ready.sem, 1)
                    act.wait_ge(diffs.sem, diffs.at(a, 2))
                    act.activation(gd[:], gd[:], ACT.Exp).then_inc(e2_ready.sem, 1)
                    act.wait_ge(diffs.sem, diffs.at(a, 3))
                    for h in range(H):
                        act.activation(sd[:, h, :], sd[:, h, :], ACT.Sigmoid, bias=neg_first[:, h:h + 1],
                                       scale=-1.0).then_inc(sg_ready.sem, 1)
                if f is not None:
                    for h in range(H):
                        act.wait_ge(pw_done.sem, pw_done.at(f, h + 1))
                        if past(f):
                            act.wait_ge(x1_ready.sem, x1_ready.at(f - 1))
                        act.activation(s1[:, h, :], pk[:, h, :], ACT.Silu, bias=vec[:, 9, h:h + 1]).then_inc(s1_ready.sem, 1)
                if a is not None:
                    for h in range(H):
                        act.wait_ge(kvr_done.sem, kvr_done.at(a, 2 * H + h + 1))
                        if past(a):
                            act.wait_ge(wkv.sem, wkv.at(a - 1))
                        act.activation(tr[:, h, :], pk[:, h, :], ACT.Tanh, scale=0.5).then_inc(tr_ready.sem, 1)
                if f is not None:
                    for h in range(H):
                        act.wait_ge(x1_ready.sem, x1_ready.at(f, h + 1))
                        if past(f):
                            act.wait_ge(moe_done.sem, moe_done.at(f - 1))
                        act.copy(x1h[:, h, :], x1[:, h, :]).then_inc(x1h_ready.sem, 1)
                    act.wait_ge(route.sem, route.at(f, 1))
                    if past(f):
                        act.wait_ge(route.sem, route.at(f - 1))
                    act.activation(th[:], gap[:], ACT.Tanh, scale=0.5 / WSCALE).then_inc(tanh_ready.sem, 1)

                    def silus(t):
                        for g in range(NG):
                            i = t * NG + g
                            act.wait_ge(expert_done.sem, expert_done.at(f, i + 1))
                            if combined.rises(f, EPG * (i + 1 - NY)):
                                act.wait_ge(combined.sem, combined.at(f, EPG * (i + 1 - NY)))
                            act.activation(ye[:, i % NY, :], pe[:, i % 2, :], ACT.Silu,
                                           scale=1.0 / WSCALE).then_inc(ye_ready.sem, 1)

                    def copy_combined(t):
                        act.wait_ge(t3_done.sem, t3_done.at(f, t + 1))
                        if past(f):
                            act.wait_ge(moe_done.sem, moe_done.at(f - 1))
                        act.copy(combt[:, :, t * P:(t + 1) * P],
                                 pt[:, t % 2, 0:C].rearrange("p (h k) -> p h k", h=H)).then_inc(combt_ready.sem, 1)

                    def squares(b):
                        act.wait_ge(moe_done.sem, moe_done.at(f, b + 1))
                        if past(f):
                            act.wait_ge(rms_ready.sem, rms_ready.at(f - 1))
                        for t in range(2 * b, 2 * b + 2):
                            if ms_ready.rises(f, t):
                                act.wait_ge(ms_ready.sem, ms_ready.at(f, t))
                            act.activation(sq[:], po[:, b, t % 2, :], ACT.Square,
                                           accum_out=ms[:, t:t + 1]).then_inc(ms_ready.sem, 1)

                    silus(0)
                    silus(1)
                    copy_combined(0)
                    silus(2)
                    copy_combined(1)
                    squares(0)
                    silus(3)
                    copy_combined(2)
                    copy_combined(3)
                if a is not None:
                    act.preload_act_table_set("natural_log_exp_and_others")
                    act.wait_ge(wkv.sem, wkv.at(a, 6))
                    act.activation(den[:], den[:], ACT.Ln, bias=one[:, 0:1]).then_inc(ln_ready.sem, 1)
                    act.wait_ge(ln_ready.sem, ln_ready.at(a))
                    act.activation(den[:], den[:], ACT.Exp, scale=-1.0).then_inc(rec_ready.sem, 1)
                if f is not None:
                    squares(1)
                    for h in range(H):
                        act.wait_ge(t4_done.sem, t4_done.at(f, h + 1))
                        if past(f):
                            act.wait_ge(down_done.sem, down_done.at(f - 1))
                        act.copy(ht[:, h, :], pt[:, h, :]).then_inc(ht_ready.sem, 1)
                    act.wait_ge(down_done.sem, down_done.at(f))
                    if past(f):
                        act.wait_ge(up_done.sem, up_done.at(f - 1))
                    act.activation(ffg[:], pk[0:HID, 1, :], ACT.Gelu, bias=bdown[:, 0:1]).then_inc(ffg_ready.sem, 1)
                if n is not None:
                    for h in range(H):
                        act.wait_ge(t1_done.sem, t1_done.at(n, h + 1))
                        if past(n):
                            act.wait_ge(mixed.sem, mixed.at(n - 1))
                        act.copy(xt1[:, h, 1:1 + T], pt[:, h, :]).then_inc(xt1_ready.sem, 1)

            schedule(act, body)

        @block.vector
        def _(dve):
            v = nc.vector
            count = [0]

            def const(ins):
                count[0] += 1
                ins.then_inc(dve_const.sem, 1)

            def const_wait():
                dve.wait_ge(dve_const.sem, count[0])

            for h in range(H):
                dve.wait_ge(stage_in.sem, 16 * (h + 1))
                const(v.tensor_scalar(weh[:, h, :], wstage, WSCALE, None, ALU.mult))
                const_wait()
                const(v.scalar_tensor_tensor(out=wel[:, h, :], in0=wstage, scalar=WSCALE, in1=weh[:, h, :],
                                             op0=ALU.mult, op1=ALU.subtract))
            dve.wait_ge(small_w_in.sem, small_w_in.per)
            dve.wait_ge(attn_w_in.sem, 16)
            const(v.tensor_scalar(wrh[:], wrout[:], WSCALE, None, ALU.mult))
            const(v.memset(row_is[:], 0.0))
            const_wait()
            const(v.scalar_tensor_tensor(out=wrl[:], in0=wrout[:], scalar=WSCALE, in1=wrh[:], op0=ALU.mult,
                                         op1=ALU.subtract))
            const(v.tensor_scalar(wo2[:], wa[:, 3], 0.5, None, ALU.mult))
            const(v.memset(row_is[:, 1:2], 1.0))
            const_wait()
            const(v.memset(row_is[0:1, 0:1], 1.0))
            const(v.memset(row_is[0:1, 1:2], 0.0))
            const(v.tensor_scalar(rows[:, 0:OB], rows[:, 0:OB], WSCALE, None, ALU.mult))
            const_wait()
            const(v.tensor_copy(brow[:], rows[:]))
            const_wait()
            const(v.tensor_tensor(rows_l[:], rows[:], brow[:], ALU.subtract))
            const_wait()
            const(v.tensor_scalar(rows_l[:], rows_l[:], row_is[:, 1:2], None, ALU.mult))
            const_wait()
            const(v.scalar_tensor_tensor(out=brow[:], in0=brow[:], scalar=row_is[:, 0:1], in1=rows_l[:],
                                         op0=ALU.mult, op1=ALU.add))
            const(v.memset(ones2[:], 1.0))
            const(v.memset(one[:], 1.0))
            for e in range(NE):
                ins = v.memset(rank[:, :, e:e + 1], float(NE - e))
            const(ins)
            for h in range(H):
                v.memset(xt1[:, h, 0:1], 0.0)
                v.memset(xt2[:, h, 0:2], 0.0)
                v.memset(pp[:, h, 0:1], NEG_INF)
                v.memset(aa[:, h, 0:1], 0.0)
                ins = v.memset(bb[:, h, 0:1], 0.0)
            const(ins)
            dve.wait_ge(pool_const.sem, 5)
            const(v.tensor_copy(ident16[:], ident[:]))
            dve.wait_ge(decay_exp.sem, 1)
            const(v.tensor_scalar(neg_first[:], vec[:, 1, :], -1.0, None, ALU.mult))
            const(v.tensor_scalar(decay[:], decay[:], -1.0, None, ALU.mult))
            assert count[0] == DVE_CONST, count[0]

            def layer_norm(seq, src, st, mo, rs, dst, stats, moments, rstd_ready, ready, turned):
                if past(seq):
                    dve.wait_ge(ready.sem, ready.at(seq - 1))
                for t in range(NT):
                    v.bn_stats(st[:, t, :], src[:, t, :]).then_inc(stats.sem, 1)
                dve.wait_ge(stats.sem, stats.at(seq))
                v.tensor_tensor(mo[:, 1], st[:, :, 1], st[:, :, 4], ALU.subtract).then_inc(moments.sem, 1)
                v.tensor_tensor(mo[:, 3], st[:, :, 2], st[:, :, 5], ALU.add).then_inc(moments.sem, 1)
                v.tensor_tensor(mo[:, 0], st[:, :, 1], st[:, :, 4], ALU.add).then_inc(moments.sem, 1)
                dve.wait_ge(moments.sem, moments.at(seq, 1))
                v.scalar_tensor_tensor(out=mo[:, 2], in0=mo[:, 1], scalar=C / 4.0, in1=mo[:, 1], op0=ALU.mult,
                                       op1=ALU.mult).then_inc(moments.sem, 1)
                dve.wait_ge(moments.sem, moments.at(seq, 3))
                v.tensor_scalar(mo[:, 0], mo[:, 0], 0.5, None, ALU.mult).then_inc(moments.sem, 1)
                dve.wait_ge(moments.sem, moments.at(seq, 4))
                v.scalar_tensor_tensor(out=mo[:, 3], in0=mo[:, 3], scalar=C * LN_EPS, in1=mo[:, 2], op0=ALU.add,
                                       op1=ALU.add).then_inc(moments.sem, 1)
                dve.wait_ge(moments.sem, moments.at(seq))
                dve.wait_ge(rstd_ready.sem, rstd_ready.at(seq))
                if past(seq):
                    dve.wait_ge(turned.sem, turned.at(seq - 1))
                for t in range(NT):
                    v.tensor_scalar(dst[:, t, :], src[:, t, :], mo[:, 0, t:t + 1], rs[:, t:t + 1], ALU.subtract,
                                    ALU.mult).then_inc(ready.sem, 1)

            def body(f, a, n):
                if f is not None:
                    for tap in (1, 2):
                        for h in range(H):
                            dve.wait_ge(tap_ready.sem, tap_ready.at(f, h + 1))
                            dve.wait_ge(xt2_ready.sem, xt2_ready.at(f, h + 1))
                            if tap == 2:
                                dve.wait_ge(conv.sem, conv.at(f, h + 1))
                            v.scalar_tensor_tensor(out=cv[:, h, :], in0=xt2[:, h, 2 - tap:2 - tap + T],
                                                   scalar=vec[:, 7 - tap, h:h + 1], in1=cv[:, h, :],
                                                   op0=ALU.mult, op1=ALU.add).then_inc(conv.sem, 1)
                if a is not None:
                    if past(a):
                        dve.wait_ge(diffs.sem, diffs.at(a - 1))
                    for h in range(H):
                        dve.wait_ge(k_ready.sem, k_ready.at(a, h + 1))
                        v.tensor_tensor_scan(pp[:, h, 1:1 + T], decay[:, h:h + 1].to_broadcast([P, T]), kk[:, h, :],
                                             NEG_INF, ALU.add, ALU.max).then_inc(p_ready.sem, 1)
                    dve.wait_ge(p_ready.sem, p_ready.at(a))
                    if past(a):
                        dve.wait_ge(wkv.sem, wkv.at(a - 1))
                    v.tensor_tensor(fd[:], pp[:, :, 0:T], pp[:, :, 1:1 + T], ALU.subtract).then_inc(diffs.sem, 1)
                    v.tensor_tensor(gd[:], kk[:], pp[:, :, 1:1 + T], ALU.subtract).then_inc(diffs.sem, 1)
                    v.tensor_tensor(sd[:], kk[:], pp[:, :, 0:T], ALU.subtract).then_inc(diffs.sem, 1)

                def wkv_step(i):
                    if i == 0:
                        dve.wait_ge(e2_ready.sem, e2_ready.at(a))
                        dve.wait_ge(v_ready.sem, v_ready.at(a))
                        v.tensor_tensor(ev[:], gd[:], vv[:], ALU.mult).then_inc(wkv.sem, 1)
                    elif i in (1, 2):
                        h = i - 1
                        dve.wait_ge(e1_ready.sem, e1_ready.at(a, h + 1))
                        dve.wait_ge(wkv.sem, wkv.at(a, 1))
                        v.tensor_tensor_scan(aa[:, h, 1:1 + T], fd[:, h, :], ev[:, h, :], 0.0, ALU.mult,
                                             ALU.add).then_inc(wkv.sem, 1)
                    elif i in (3, 4):
                        h = i - 3
                        v.tensor_tensor_scan(bb[:, h, 1:1 + T], fd[:, h, :], gd[:, h, :], 0.0, ALU.mult,
                                             ALU.add).then_inc(wkv.sem, 1)
                    elif i == 5:
                        dve.wait_ge(sg_ready.sem, sg_ready.at(a))
                        dve.wait_ge(wkv.sem, wkv.at(a, 5))
                        v.scalar_tensor_tensor(out=den[:], in0=bb[:, :, 0:T], scalar=1.0, in1=sd[:],
                                               op0=ALU.subtract, op1=ALU.mult).then_inc(wkv.sem, 1)
                    elif i == 6:
                        v.tensor_tensor(num[:], aa[:, :, 0:T], vv[:], ALU.subtract).then_inc(wkv.sem, 1)
                    elif i == 7:
                        dve.wait_ge(wkv.sem, wkv.at(a, 7))
                        v.tensor_tensor(num[:], num[:], sd[:], ALU.mult).then_inc(wkv.sem, 1)
                    elif i == 8:
                        dve.wait_ge(wkv.sem, wkv.at(a, 8))
                        v.tensor_tensor(num[:], num[:], vv[:], ALU.add).then_inc(wkv.sem, 1)
                    elif i == 9:
                        dve.wait_ge(wkv.sem, wkv.at(a, 9))
                        dve.wait_ge(tr_ready.sem, tr_ready.at(a))
                        v.scalar_tensor_tensor(out=num[:], in0=tr[:], scalar=1.0, in1=num[:], op0=ALU.add,
                                               op1=ALU.mult).then_inc(wkv.sem, 1)
                    elif i == 10:
                        dve.wait_ge(wkv.sem, wkv.at(a, 10))
                        dve.wait_ge(rec_ready.sem, rec_ready.at(a))
                        if past(a):
                            dve.wait_ge(wo_done.sem, wo_done.at(a - 1))
                        v.tensor_tensor(rwkv[:], num[:], den[:], ALU.mult).then_inc(wkv.sem, 1)

                if f is not None:
                    for h in range(H):
                        dve.wait_ge(s1_ready.sem, s1_ready.at(f, h + 1))
                        if past(f):
                            dve.wait_ge(x1h_ready.sem, x1h_ready.at(f - 1))
                        if past(f):
                            dve.wait_ge(x1l_ready.sem, x1l_ready.at(f - 1))
                        v.tensor_tensor(x1[:, h, :], s1[:, h, :], xt2[:, h, 2:2 + T], ALU.add).then_inc(x1_ready.sem, 1)
                    for h in range(H):
                        dve.wait_ge(x1_ready.sem, x1_ready.at(f, h + 1))
                        dve.wait_ge(x1h_ready.sem, x1h_ready.at(f, h + 1))
                        if past(f):
                            dve.wait_ge(moe_done.sem, moe_done.at(f - 1))
                        v.tensor_tensor(x1l[:, h, :], x1[:, h, :], x1h[:, h, :], ALU.subtract).then_inc(x1l_ready.sem, 1)
                    if a is not None:
                        wkv_step(0)
                    wide = lambda x: x.unsqueeze(2).to_broadcast([P, NT, NE])
                    dve.wait_ge(routed.sem, routed.at(f))
                    if past(f):
                        dve.wait_ge(route.sem, route.at(f - 1))
                    v.tensor_copy(lg[:], pk[:, 0, 0:NT * NE].rearrange("p (t e) -> p t e", e=NE)).then_inc(logits_read.sem, 1)
                    dve.wait_ge(logits_read.sem, logits_read.at(f))
                    for j, src in ((0, lg), (1, lg2)):
                        if j == 1:
                            dve.wait_ge(picks.sem, picks.at(f, 5))
                            v.scalar_tensor_tensor(out=lg2[:], in0=sel[:, 0], scalar=NEG_INF, in1=lg[:], op0=ALU.mult,
                                                   op1=ALU.add).then_inc(picks.sem, 1)
                            dve.wait_ge(picks.sem, picks.at(f, 6))
                        v.tensor_reduce(top[:, j], src[:], AX_X, ALU.max).then_inc(picks.sem, 1)
                        dve.wait_ge(picks.sem, picks.at(f, 6 * j + 1))
                        v.tensor_tensor(hit[:, j], src[:], wide(top[:, j]), ALU.is_equal).then_inc(picks.sem, 1)
                        dve.wait_ge(picks.sem, picks.at(f, 6 * j + 2))
                        v.tensor_tensor(hit[:, j], hit[:, j], rank[:], ALU.mult).then_inc(picks.sem, 1)
                        dve.wait_ge(picks.sem, picks.at(f, 6 * j + 3))
                        v.tensor_reduce(first[:, j], hit[:, j], AX_X, ALU.max).then_inc(picks.sem, 1)
                        dve.wait_ge(picks.sem, picks.at(f, 6 * j + 4))
                        v.tensor_tensor(sel[:, j], rank[:], wide(first[:, j]), ALU.is_equal).then_inc(picks.sem, 1)
                    v.tensor_tensor(gap[:], top[:, 0], top[:, 1], ALU.subtract).then_inc(route.sem, 1)
                    dve.wait_ge(tanh_ready.sem, tanh_ready.at(f))
                    if past(f):
                        dve.wait_ge(combined.sem, combined.at(f - 1))
                    for j, s in ((0, 0.5), (1, -0.5)):
                        v.tensor_scalar(w12[:, j, :], th[:], s, 0.5, ALU.mult, ALU.add).then_inc(route.sem, 1)
                    dve.wait_ge(picks.sem, picks.at(f))
                    dve.wait_ge(route.sem, route.at(f, 3))
                    v.tensor_tensor(sel[:], sel[:], w12[:].unsqueeze(3).to_broadcast([P, 2, NT, NE]),
                                    ALU.mult).then_inc(route.sem, 1)
                    dve.wait_ge(route.sem, route.at(f, 4))
                    v.tensor_tensor(rw[:], sel[:, 0], sel[:, 1], ALU.add).then_inc(route.sem, 1)
                    dve.wait_ge(route.sem, route.at(f, 5))
                    for t in range(NT):
                        for g in range(NG):
                            i = t * NG + g
                            dve.wait_ge(ye_ready.sem, ye_ready.at(f, i + 1))
                            for k in range(EPG):
                                e = g * EPG + k
                                src = ye[:, i % NY, k * C:(k + 1) * C]
                                if e == 0:
                                    if past(f):
                                        dve.wait_ge(t3_done.sem, t3_done.at(f - 1, t + 1))
                                    ins = v.tensor_scalar(comb[:, t, :], src, rw[:, t, 0:1], None, ALU.mult)
                                else:
                                    dve.wait_ge(combined.sem, combined.at(f, t * NE + e))
                                    ins = v.scalar_tensor_tensor(out=comb[:, t, :], in0=src, scalar=rw[:, t, e:e + 1],
                                                                 in1=comb[:, t, :], op0=ALU.mult, op1=ALU.add)
                                ins.then_inc(combined.sem, 1)
                            if a is not None and 1 <= i <= 9:
                                wkv_step(i)
                elif a is not None:
                    for i in range(10):
                        wkv_step(i)
                if a is not None:
                    wkv_step(10)
                if f is not None:
                    for b in range(2):
                        dve.wait_ge(rms_ready.sem, rms_ready.at(f, 3 * b + 3))
                        if past(f):
                            dve.wait_ge(t4_done.sem, t4_done.at(f - 1))
                        if past(f):
                            dve.wait_ge(xh_ready.sem, xh_ready.at(f - 1))
                        for t in range(2 * b, 2 * b + 2):
                            v.scalar_tensor_tensor(out=hh[:, t, :], in0=po[:, b, t % 2, :], scalar=rms[:, t:t + 1],
                                                   in1=normw[:], op0=ALU.mult, op1=ALU.mult).then_inc(h_ready.sem, 1)
                    if past(f):
                        dve.wait_ge(y_ready.sem, y_ready.at(f - 1))
                    for b in range(2):
                        dve.wait_ge(h_ready.sem, h_ready.at(f, 2 * b + 2))
                        t = slice(2 * b, 2 * b + 2)
                        v.tensor_tensor(xh[:, t, :], x2[:, t, :], hh[:, t, :], ALU.add).then_inc(xh_ready.sem, 1)
                if n is not None:
                    dve.wait_ge(x_in.sem, x_in.at(n))
                    layer_norm(n, xa, st1, mo1, rstd1, xn1, stats1, moments1, rstd1_ready, xn1_ready, t1_done)
                if a is not None:
                    dve.wait_ge(xres_in.sem, xres_in.at(a))
                    if past(a):
                        dve.wait_ge(xn2_ready.sem, xn2_ready.at(a - 1))
                    if past(a):
                        dve.wait_ge(xh_ready.sem, xh_ready.at(a - 1))
                    for b in range(2):
                        dve.wait_ge(wo_done.sem, wo_done.at(a, b + 1))
                        t = slice(2 * b, 2 * b + 2)
                        v.tensor_tensor(x2[:, t, :], po[:, b], xres[:, t, :], ALU.add).then_inc(x2_ready.sem, 1)
                    dve.wait_ge(x2_ready.sem, x2_ready.at(a))
                    layer_norm(a, x2, st2, mo2, rstd2, xn2, stats2, moments2, rstd2_ready, xn2_ready, t2_done)
                if n is not None:
                    dve.wait_ge(xt1_ready.sem, xt1_ready.at(n))
                    if past(n):
                        dve.wait_ge(mixed.sem, mixed.at(n - 1))
                    if past(n):
                        dve.wait_ge(kvr_done.sem, kvr_done.at(n - 1))
                    v.tensor_tensor(xd[:], xt1[:, :, 1:1 + T], xt1[:, :, 0:T], ALU.subtract).then_inc(mixed.sem, 1)
                    dve.wait_ge(mixed.sem, mixed.at(n, 1))
                    for m, dst in ((2, xk), (3, xv), (4, xr)):
                        for h in range(H):
                            v.scalar_tensor_tensor(out=dst[:, h, :], in0=xd[:, h, :], scalar=vec[:, m, h:h + 1],
                                                   in1=xt1[:, h, 0:T], op0=ALU.mult, op1=ALU.add).then_inc(mixed.sem, 1)
                if f is not None:
                    if past(f):
                        dve.wait_ge(stored.sem, stored.at(f - 1))
                    dve.wait_ge(xh_ready.sem, xh_ready.at(f))
                    for b in range(2):
                        dve.wait_ge(up_done.sem, up_done.at(f, b + 1))
                        t = slice(2 * b, 2 * b + 2)
                        v.tensor_tensor(yo[:, t, :], po[:, b], xh[:, t, :], ALU.add).then_inc(y_ready.sem, 1)

            schedule(dve, body)


def kernel(**inputs):
    import numpy as np
    import concourse.bacc as bacc
    from concourse.bass_utils import run_bass_kernel_spmd

    g = {k: np.asarray(v) for k, v in inputs.items()}
    C = g["L0_attn_x"].shape[2]
    conv = g["L0_ffn_dw_kernel"]
    vectors = [g["L0_attn_time_decay"], g["L0_attn_time_first"], g["L0_attn_time_mix_k"].reshape(C),
               g["L0_attn_time_mix_v"].reshape(C), g["L0_attn_time_mix_r"].reshape(C), conv[:, 0, 0], conv[:, 0, 1],
               conv[:, 0, 2], g["L0_ffn_dw_bias"], g["L0_ffn_pw_b"]]
    arrays = {
        "in_x": g["L0_attn_x"],
        "in_vecs": np.stack([v.reshape(C // P, P).T for v in vectors], axis=1),
        "in_w_attn": np.stack([g["L0_attn_" + n].T for n in ("Wk", "Wv", "Wr", "Wo")]),
        "in_w_pw": g["L0_ffn_pw_w"].T,
        "in_w_router": g["L0_ffn_router_w"].T,
        "in_w_expert": g["L0_ffn_expert_w"].transpose(2, 0, 1).reshape(C, -1),
        "in_w_out": g["L0_ffn_out_w"].T,
        "in_w_down": g["L0_ffn_ff_down_w"].T,
        "in_w_up": g["L0_ffn_ff_up_w"].T,
        "in_b_rows": np.concatenate([g["L0_ffn_expert_b"].reshape(-1), g["L0_ffn_router_b"], g["L0_ffn_out_b"],
                                     g["L0_ffn_ff_up_b"]])[None, :],
        "in_b_down": g["L0_ffn_ff_down_b"][:, None],
        "in_norm_w": g["L0_ffn_norm_w"][None, :],
    }
    arrays = {k: np.ascontiguousarray(v) for k, v in arrays.items()}
    nc = bacc.Bacc("TRN2", target_bir_lowering=False, num_devices=1)
    args = [nc.dram_tensor(k, v.shape, mybir.dt.from_np(v.dtype), kind="ExternalInput").ap() for k, v in arrays.items()]
    shape = g["L0_attn_x"].shape
    out = nc.dram_tensor("out_y", shape, F32, kind="ExternalOutput").ap()
    build(nc, *args, out)
    r = run_bass_kernel_spmd(nc, [arrays], core_ids=[0])
    return r.results[0]["out_y"]
```

```python
from contextlib import ExitStack

import concourse.bass as bass
from concourse import mybir

F32 = mybir.dt.float32
F16 = mybir.dt.float16
AX_X = mybir.AxisListType.X
ALU = mybir.AluOpType
ACT = mybir.ActivationFunctionType

P = 128
NEG_INF = -1e38
LN_EPS = 1e-5
RMS_EPS = 1e-6
WSCALE = 64.0

VECS = ["time_decay", "time_first", "mix_k", "mix_v", "mix_r", "conv0", "conv1", "conv2", "conv_b", "pw_b"]


class Signal:

    def __init__(self, sem, per):
        self.sem, self.per = sem, per

    def at(self, seq, n=None):
        return self.per * seq + (self.per if n is None else n)

    def rises(self, seq, n):
        value = self.at(seq, n)
        return not isinstance(value, int) or value > 0


def build(nc, x, vecs, w_attn, w_pw, w_router, w_expert, w_out, w_down, w_up, b_rows, b_down, norm_w, out):
    B, T, C = x.shape
    H = C // P
    NT = T // P
    NE = w_router.shape[1]
    HID = w_down.shape[1]
    NG = NE * C // T
    EPG = NE // NG
    RB, OB, UB = NE * C, NE * C + NE, NE * C + NE + C
    NROW = UB + C
    NV = len(VECS)

    with ExitStack() as ctx:
        def sb(name, shape, dt=F32):
            return ctx.enter_context(nc.sbuf_tensor(name, shape, dt))

        def ps(name, shape):
            return ctx.enter_context(nc.psum_tensor(name, shape, F32))

        def sig(name, per):
            return Signal(ctx.enter_context(nc.semaphore(name)), per)

        vec = sb("vec", [P, NV, H])
        decay = sb("decay", [P, H])
        neg_first = sb("neg_first", [P, H])
        wa = sb("wa", [P, 4, H, C])
        wpw = sb("wpw", [P, H, C])
        wo2 = sb("wo2", [P, H, C])
        wout = sb("wout", [P, H, C])
        wdown = sb("wdown", [P, H, HID])
        wup = sb("wup", [HID, C])
        bdown = sb("bdown", [HID, 1])
        wrout = sb("wrout", [P, H, NE])
        wrh = sb("wrh", [P, H, NE], F16)
        wrl = sb("wrl", [P, H, NE], F16)
        weh = sb("weh", [P, H, NE * C], F16)
        wel = sb("wel", [P, H, NE * C], F16)
        rows = sb("rows", [2, NROW])
        rows_l = sb("rows_l", [2, NROW], F16)
        brow = sb("brow", [2, NROW], F16)
        row_is = sb("row_is", [2, 2])
        ones2 = sb("ones2", [2, P], F16)
        one = sb("one", [P, 1])
        normw = sb("normw", [P, C])
        ident = sb("ident", [P, P])
        ident16 = sb("ident16", [P, P], F16)
        rank = sb("rank", [P, NT, NE])
        minus_half = sb("minus_half", [P, NT])
        sqrt_c = sb("sqrt_c", [P, NT])
        rms_eps_c = sb("rms_eps_c", [P, NT])

        xa = sb("xa", [P, NT, C])
        st1 = sb("st1", [P, NT, 6])
        mo1 = sb("mo1", [P, 4, NT])
        pw1 = sb("pw1", [P, NT])
        rstd1 = sb("rstd1", [P, NT])
        xn1 = sb("xn1", [P, NT, C])
        xt1 = sb("xt1", [P, H, 1 + T])
        xd = sb("xd", [P, H, T])
        xk = sb("xk", [P, H, T])
        xv = sb("xv", [P, H, T])
        xr = sb("xr", [P, H, T])
        kk = sb("kk", [P, H, T])
        vv = sb("vv", [P, H, T])
        pp = sb("pp", [P, H, 1 + T])
        fd = sb("fd", [P, H, T])
        gd = sb("gd", [P, H, T])
        sd = sb("sd", [P, H, T])
        ev = sb("ev", [P, H, T])
        aa = sb("aa", [P, H, 1 + T])
        bb = sb("bb", [P, H, 1 + T])
        num = sb("num", [P, H, T])
        den = sb("den", [P, H, T])
        tr = sb("tr", [P, H, T])
        rwkv = sb("rwkv", [P, H, T])
        xres = sb("xres", [P, NT, C])
        x2 = sb("x2", [P, NT, C])
        x2t = sb("x2t", [P, NT, C])
        st2 = sb("st2", [P, NT, 6])
        mo2 = sb("mo2", [P, 4, NT])
        pw2 = sb("pw2", [P, NT])
        rstd2 = sb("rstd2", [P, NT])
        xn2 = sb("xn2", [P, NT, C])
        xt2 = sb("xt2", [P, H, 2 + T])
        cv = sb("cv", [P, H, T])
        x1 = sb("x1", [P, H, T])
        x1h = sb("x1h", [P, H, T], F16)
        x1l = sb("x1l", [P, H, T], F16)
        lg = sb("lg", [P, NT, NE])
        lg2 = sb("lg2", [P, NT, NE])
        hit = sb("hit", [P, 2, NT, NE])
        top = sb("top", [P, 2, NT])
        first = sb("first", [P, 2, NT])
        gap = sb("gap", [P, NT])
        th = sb("th", [P, NT])
        w12 = sb("w12", [P, 2, NT])
        sel = sb("sel", [P, 2, NT, NE])
        rw = sb("rw", [P, NT, NE])
        NY = 4
        ye = sb("ye", [P, NY, T])
        wstage = ye[:].rearrange("p y t -> p (y t)")
        comb = sb("comb", [P, NT, C])
        combt = sb("combt", [P, H, T])
        sq = sb("sq", [P, C])
        ms = sb("ms", [P, NT])
        msv = sb("msv", [P, NT])
        msp = sb("msp", [P, NT])
        rms = sb("rms", [P, NT])
        hh = sb("hh", [P, NT, C])
        ht = sb("ht", [P, H, T])
        xh = sb("xh", [P, NT, C])
        ffg = sb("ffg", [HID, T])
        yo = sb("yo", [P, NT, C])

        pt = ps("pt", [P, 2, T])
        pk = ps("pk", [P, 2, T])
        pe = ps("pe", [P, 2, T])
        po = ps("po", [P, 2, 2, C])

        vecs_in = sig("vecs_in", 16)
        attn_w_in = sig("attn_w_in", 16)
        small_w_in = sig("small_w_in", 16 * 9)
        stage_in = sig("stage_in", 16)
        decay_exp = sig("decay_exp", 1)
        pool_const = sig("pool_const", 5)
        early_const = sig("early_const", 1)
        dve_const = sig("dve_const", 1)
        x_in = sig("x_in", 16)
        stats1 = sig("stats1", NT)
        moments1 = sig("moments1", 6)
        rstd1_ready = sig("rstd1_ready", 2)
        xn1_ready = sig("xn1_ready", NT)
        t1_done = sig("t1_done", 2)
        xt1_ready = sig("xt1_ready", 2)
        mixed = sig("mixed", 7)
        kvr_done = sig("kvr_done", 6)
        k_ready = sig("k_ready", 2)
        v_ready = sig("v_ready", 2)
        tr_ready = sig("tr_ready", 2)
        p_ready = sig("p_ready", 2)
        diffs = sig("diffs", 3)
        e1_ready = sig("e1_ready", 2)
        e2_ready = sig("e2_ready", 1)
        sg_ready = sig("sg_ready", 2)
        wkv = sig("wkv", 10)
        rwkv_ready = sig("rwkv_ready", 1)
        ln_ready = sig("ln_ready", 1)
        rec_ready = sig("rec_ready", 1)
        wo_done = sig("wo_done", 2)
        xres_in = sig("xres_in", 16)
        x2_ready = sig("x2_ready", 2)
        stats2 = sig("stats2", NT)
        moments2 = sig("moments2", 6)
        rstd2_ready = sig("rstd2_ready", 2)
        xn2_ready = sig("xn2_ready", NT)
        t2_done = sig("t2_done", 2)
        xt2_ready = sig("xt2_ready", 2)
        tap_ready = sig("tap_ready", 2)
        conv = sig("conv", 4)
        pw_done = sig("pw_done", 2)
        s1_ready = sig("s1_ready", 2)
        x1_ready = sig("x1_ready", 2)
        x1h_ready = sig("x1h_ready", 2)
        x1l_ready = sig("x1l_ready", 2)
        routed = sig("routed", 1)
        logits_read = sig("logits_read", 1)
        picks = sig("picks", 11)
        route = sig("route", 5)
        tanh_ready = sig("tanh_ready", 1)
        expert_done = sig("expert_done", NT * NG)
        ye_ready = sig("ye_ready", NT * NG)
        combined = sig("combined", NT * NE)
        t3_done = sig("t3_done", NT)
        combt_ready = sig("combt_ready", NT)
        moe_done = sig("moe_done", 2)
        ms_ready = sig("ms_ready", NT)
        rms_ready = sig("rms_ready", 6)
        h_ready = sig("h_ready", NT)
        xh_ready = sig("xh_ready", 1)
        x2t_ready = sig("x2t_ready", 1)
        t4_done = sig("t4_done", 2)
        ht_ready = sig("ht_ready", 2)
        down_done = sig("down_done", 1)
        ffg_ready = sig("ffg_ready", 1)
        up_done = sig("up_done", 2)
        y_ready = sig("y_ready", 2)
        stored = sig("stored", 16)

        x_tok = x.rearrange("b (t p) c -> b p t c", p=P)
        out_tok = out.rearrange("b (t p) c -> b p t c", p=P)
        WKV_AT = {3: 5, 5: 6, 7: 7, 8: 8, 10: 9}
        EARLY_CONST = 4
        DVE_CONST = 15 + 2 * H

        def on(seq):
            return not isinstance(seq, int) or 0 <= seq < B

        def dram_seq(ap, seq):
            return ap[bass.ds(seq, 1)].rearrange("a p t c -> p (a t) c")

        def schedule(eng, body, between=None):
            for g in range(-4, 1):
                body(g, g + 1, g + 2, g + 3, g + 4)
                if g == -4 and between is not None:
                    between()
            with eng.Fori(1, B - 5) as g:
                body(g, g + 1, g + 2, g + 3, g + 4)
            for g in range(B - 5, B):
                body(g, g + 1, g + 2, g + 3, g + 4)

        block = ctx.enter_context(nc.Block())

        @block.sync
        def _(sp):
            halves = lambda w: w.rearrange("(h p) c -> p h c", p=P)
            sp.dma_start(xa[:], dram_seq(x_tok, 0)).then_inc(x_in.sem, 16)
            sp.dma_start(vec[:], vecs).then_inc(vecs_in.sem, 16)
            sp.dma_start(wa[:], w_attn.rearrange("m (h p) c -> p m h c", p=P)).then_inc(attn_w_in.sem, 16)
            sp.dma_start(wstage, w_expert[0:P, :]).then_inc(stage_in.sem, 16)
            sp.dma_start(wpw[:], halves(w_pw)).then_inc(small_w_in.sem, 16)
            sp.dma_start(wrout[:], halves(w_router)).then_inc(small_w_in.sem, 16)
            sp.dma_start(wout[:], halves(w_out)).then_inc(small_w_in.sem, 16)
            sp.dma_start(wdown[:], halves(w_down)).then_inc(small_w_in.sem, 16)
            sp.dma_start(wup[:], w_up).then_inc(small_w_in.sem, 16)
            sp.dma_start(bdown[:], b_down).then_inc(small_w_in.sem, 16)
            sp.dma_start(normw[:], norm_w.to_broadcast([P, C])).then_inc(small_w_in.sem, 16)
            for row in range(2):
                sp.dma_start(rows[row:row + 1, :], b_rows).then_inc(small_w_in.sem, 16)

            def body(g, f, b, a, n):
                if on(n + 1):
                    if on(n):
                        sp.wait_ge(xn1_ready.sem, xn1_ready.at(n))
                    sp.dma_start(xa[:], dram_seq(x_tok, n + 1)).then_inc(x_in.sem, 16)
                if on(a):
                    if on(b):
                        sp.wait_ge(x2_ready.sem, x2_ready.at(b))
                    sp.dma_start(xres[:], dram_seq(x_tok, a)).then_inc(xres_in.sem, 16)
                if on(g):
                    sp.wait_ge(y_ready.sem, y_ready.at(g))
                    sp.dma_start(dram_seq(out_tok, g), yo[:]).then_inc(stored.sem, 16)

            def second_half():
                for h in range(1, H):
                    sp.wait_ge(dve_const.sem, 2 * h)
                    sp.dma_start(wstage, w_expert[h * P:(h + 1) * P, :]).then_inc(stage_in.sem, 16)

            schedule(sp, body, second_half)
            sp.wait_ge(stored.sem, stored.at(B - 1))

        @block.gpsimd
        def _(pool):
            nc.gpsimd.memset(ident[:], 0.0).then_inc(pool_const.sem, 1)
            pool.wait_ge(pool_const.sem, 1)
            nc.gpsimd.affine_select(out=ident[:], in_=ident[:], compare_op=ALU.not_equal, fill=1.0, base=0,
                                    pattern=[[-1, P]], channel_multiplier=1).then_inc(pool_const.sem, 1)
            nc.gpsimd.memset(minus_half[:], -0.5).then_inc(pool_const.sem, 1)
            nc.gpsimd.memset(sqrt_c[:], float(C) ** 0.5).then_inc(pool_const.sem, 1)
            nc.gpsimd.memset(rms_eps_c[:], RMS_EPS * C).then_inc(pool_const.sem, 1)
            pool.wait_ge(pool_const.sem, 5)

            def rstd(seq, mo, pw, dst, moments, ready, used):
                pool.wait_ge(moments.sem, moments.at(seq))
                if on(seq - 1):
                    pool.wait_ge(ready.sem, ready.at(seq - 1))
                    pool.wait_ge(used.sem, used.at(seq - 1))
                nc.gpsimd.tensor_tensor(pw[:], mo[:, 3], minus_half[:], ALU.pow).then_inc(ready.sem, 1)
                pool.wait_ge(ready.sem, ready.at(seq, 1))
                nc.gpsimd.tensor_tensor(dst[:], pw[:], sqrt_c[:], ALU.mult).then_inc(ready.sem, 1)

            def inverse_rms(seq, i):
                t = slice(2 * i, 2 * i + 2)
                pool.wait_ge(ms_ready.sem, ms_ready.at(seq, 2 * i + 2))
                if on(seq - 1):
                    pool.wait_ge(rms_ready.sem, rms_ready.at(seq - 1))
                    pool.wait_ge(h_ready.sem, h_ready.at(seq - 1))
                nc.gpsimd.tensor_tensor(msv[:, t], ms[:, t], rms_eps_c[:, t], ALU.add).then_inc(rms_ready.sem, 1)
                pool.wait_ge(rms_ready.sem, rms_ready.at(seq, 3 * i + 1))
                nc.gpsimd.tensor_tensor(msp[:, t], msv[:, t], minus_half[:, t], ALU.pow).then_inc(rms_ready.sem, 1)
                pool.wait_ge(rms_ready.sem, rms_ready.at(seq, 3 * i + 2))
                nc.gpsimd.tensor_tensor(rms[:, t], msp[:, t], sqrt_c[:, t], ALU.mult).then_inc(rms_ready.sem, 1)

            def body(g, f, b, a, n):
                if on(g):
                    inverse_rms(g, 1)
                if on(n):
                    rstd(n, mo1, pw1, rstd1, moments1, rstd1_ready, xn1_ready)
                if on(b):
                    rstd(b, mo2, pw2, rstd2, moments2, rstd2_ready, xn2_ready)
                if on(f):
                    inverse_rms(f, 0)

            schedule(pool, body)

        @block.tensor
        def _(te):
            def transpose_all(src, done):
                for h in range(H):
                    for t in range(NT):
                        mm = nc.tensor.transpose(pt[:, h, t * P:(t + 1) * P], src[:, t, h * P:(h + 1) * P], ident[:])
                    mm.then_inc(done.sem, 1)

            def product(dst, weight, m, src, done):
                for h in range(H):
                    mm = nc.tensor.matmul(dst, weight[:, h, m * P:(m + 1) * P], src[:, h, :],
                                          start=h == 0, stop=h == H - 1)
                mm.then_inc(done.sem, 1)

            def body(g, f, b, a, n):
                def experts(t):
                    tok = slice(t * P, (t + 1) * P)
                    for grp in range(NG):
                        i = t * NG + grp
                        if ye_ready.rises(f, i - 1):
                            te.wait_ge(ye_ready.sem, ye_ready.at(f, i - 1))
                        dst, cols = pe[:, i % 2, :], slice(grp * T, (grp + 1) * T)
                        nc.tensor.matmul(dst, ones2[:], brow[:, cols], start=True, stop=False)
                        for h in range(H):
                            nc.tensor.matmul(dst, x1h[:, h, tok], weh[:, h, cols], start=False, stop=False)
                            nc.tensor.matmul(dst, x1h[:, h, tok], wel[:, h, cols], start=False, stop=False)
                            mm = nc.tensor.matmul(dst, x1l[:, h, tok], weh[:, h, cols], start=False, stop=h == H - 1)
                        mm.then_inc(expert_done.sem, 1)

                def turn_combined(seq, t):
                    te.wait_ge(combined.sem, combined.at(seq, NE * (t + 1)))
                    if t < 2:
                        if on(n):
                            te.wait_ge(xt1_ready.sem, xt1_ready.at(n, t + 1))
                        if on(g):
                            te.wait_ge(ffg_ready.sem, ffg_ready.at(g))
                    else:
                        te.wait_ge(combt_ready.sem, combt_ready.at(seq, t - 1))
                        if on(seq + 1):
                            te.wait_ge(xt2_ready.sem, xt2_ready.at(seq + 1, t - 1))
                    for h in range(H):
                        mm = nc.tensor.transpose(pt[:, t % 2, h * P:(h + 1) * P], comb[:, t, h * P:(h + 1) * P],
                                                 ident[:])
                    mm.then_inc(t3_done.sem, 1)

                def mix_out(seq, i):
                    if on(seq + 1):
                        te.wait_ge(x2_ready.sem, x2_ready.at(seq + 1, i + 1))
                    if on(seq - 1):
                        te.wait_ge(y_ready.sem, y_ready.at(seq - 1, i + 1))
                    for t in range(2 * i, 2 * i + 2):
                        tok = slice(t * P, (t + 1) * P)
                        te.wait_ge(combt_ready.sem, combt_ready.at(seq, t + 1))
                        dst = po[:, i, t % 2, :]
                        nc.tensor.matmul(dst, ones2[:], brow[:, OB:OB + C], start=True, stop=False)
                        for h in range(H):
                            part = dst[:, h * P:(h + 1) * P]
                            nc.tensor.matmul(part, x1h[:, h, tok], ident16[:], start=False, stop=False)
                            nc.tensor.matmul(part, x1l[:, h, tok], ident16[:], start=False, stop=False)
                        for h in range(H):
                            mm = nc.tensor.matmul(dst, combt[:, h, tok], wout[:, h, :], start=False, stop=h == H - 1)
                    mm.then_inc(moe_done.sem, 1)

                def turn_front():
                    te.wait_ge(xn1_ready.sem, xn1_ready.at(n))
                    if on(g):
                        te.wait_ge(ffg_ready.sem, ffg_ready.at(g))
                    if on(a):
                        te.wait_ge(xt1_ready.sem, xt1_ready.at(a))
                    if on(f):
                        te.wait_ge(xt2_ready.sem, xt2_ready.at(f))
                    transpose_all(xn1, t1_done)

                def project():
                    te.wait_ge(rwkv_ready.sem, rwkv_ready.at(b))
                    for i in range(2):
                        if on(g):
                            te.wait_ge(h_ready.sem, h_ready.at(g, 2 * i + 2))
                        if on(f):
                            te.wait_ge(x2_ready.sem, x2_ready.at(f, i + 1))
                        for t in range(2 * i, 2 * i + 2):
                            for h in range(H):
                                mm = nc.tensor.matmul(po[:, i, t % 2, :], rwkv[:, h, t * P:(t + 1) * P], wo2[:, h, :],
                                                      start=h == 0, stop=h == H - 1)
                        mm.then_inc(wo_done.sem, 1)

                def turn_proj():
                    te.wait_ge(xn2_ready.sem, xn2_ready.at(b))
                    if on(f):
                        te.wait_ge(combt_ready.sem, combt_ready.at(f, 2))
                    if on(n):
                        te.wait_ge(xt1_ready.sem, xt1_ready.at(n))
                    transpose_all(xn2, t2_done)

                def feed_up():
                    te.wait_ge(ffg_ready.sem, ffg_ready.at(g))
                    for i in range(2):
                        if on(b):
                            te.wait_ge(x2_ready.sem, x2_ready.at(b, i + 1))
                        for t in range(2 * i, 2 * i + 2):
                            dst = po[:, i, t % 2, :]
                            nc.tensor.matmul(dst, ones2[:], brow[:, UB:UB + C], start=True, stop=False)
                            mm = nc.tensor.matmul(dst, ffg[:, t * P:(t + 1) * P], wup[:], start=False, stop=True)
                        mm.then_inc(up_done.sem, 1)

                if on(a):
                    te.wait_ge(mixed.sem, mixed.at(a, 3))
                    for half in range(H):
                        if on(b):
                            te.wait_ge(tr_ready.sem, tr_ready.at(b, half + 1))
                        if on(g):
                            te.wait_ge(s1_ready.sem, s1_ready.at(g, half + 1))
                            te.wait_ge(logits_read.sem, logits_read.at(g))
                        product(pk[:, half, :], wa[:, 0], half, xk, kvr_done)
                if on(g):
                    turn_combined(g, 2)
                    turn_combined(g, 3)
                if on(a):
                    te.wait_ge(mixed.sem, mixed.at(a, 5))
                    for half in range(H):
                        te.wait_ge(k_ready.sem, k_ready.at(a, half + 1))
                        product(pk[:, half, :], wa[:, 1], half, xv, kvr_done)
                if on(g):
                    mix_out(g, 1)
                if on(a):
                    te.wait_ge(mixed.sem, mixed.at(a))
                    for half in range(H):
                        te.wait_ge(v_ready.sem, v_ready.at(a, half + 1))
                        product(pk[:, half, :], wa[:, 2], half, xr, kvr_done)
                if on(g):
                    te.wait_ge(h_ready.sem, h_ready.at(g))
                    te.wait_ge(combt_ready.sem, combt_ready.at(g))
                    if on(f):
                        te.wait_ge(xt2_ready.sem, xt2_ready.at(f))
                    if on(a):
                        te.wait_ge(xt1_ready.sem, xt1_ready.at(a))
                    transpose_all(hh, t4_done)
                if on(f):
                    te.wait_ge(conv.sem, conv.at(f))
                    for half in range(H):
                        if on(a):
                            te.wait_ge(tr_ready.sem, tr_ready.at(a, half + 1))
                        else:
                            te.wait_ge(logits_read.sem, logits_read.at(g))
                            if on(b):
                                te.wait_ge(tr_ready.sem, tr_ready.at(b, half + 1))
                        product(pk[:, half, :], wpw, half, cv, pw_done)
                if on(g):
                    te.wait_ge(ht_ready.sem, ht_ready.at(g))
                    for h in range(H):
                        mm = nc.tensor.matmul(pt[0:HID, 0, :], wdown[:, h, :], ht[:, h, :], start=h == 0,
                                              stop=h == H - 1)
                    mm.then_inc(down_done.sem, 1)
                if on(b):
                    project()
                if on(f):
                    te.wait_ge(x1h_ready.sem, x1h_ready.at(f))
                    te.wait_ge(x1l_ready.sem, x1l_ready.at(f))
                    te.wait_ge(s1_ready.sem, s1_ready.at(f, 1))
                    for t in range(NT):
                        tok = slice(t * P, (t + 1) * P)
                        dst = pk[:, 0, t * NE:(t + 1) * NE]
                        nc.tensor.matmul(dst, ones2[:], brow[:, RB:RB + NE], start=True, stop=False)
                        for h in range(H):
                            nc.tensor.matmul(dst, x1h[:, h, tok], wrh[:, h, :], start=False, stop=False)
                            nc.tensor.matmul(dst, x1h[:, h, tok], wrl[:, h, :], start=False, stop=False)
                            mm = nc.tensor.matmul(dst, x1l[:, h, tok], wrh[:, h, :], start=False, stop=h == H - 1)
                    mm.then_inc(routed.sem, 1)
                    experts(0)
                if on(g):
                    feed_up()
                if on(n):
                    turn_front()
                if on(f):
                    experts(1)
                    turn_combined(f, 0)
                    experts(2)
                    turn_combined(f, 1)
                    mix_out(f, 0)
                if on(b):
                    turn_proj()
                if on(f):
                    experts(3)

            def rest_of_weights():
                te.wait_ge(attn_w_in.sem, 16)
                te.wait_ge(small_w_in.sem, small_w_in.per)
                te.wait_ge(dve_const.sem, DVE_CONST)

            te.wait_ge(pool_const.sem, 5)
            te.wait_ge(early_const.sem, EARLY_CONST)
            schedule(te, body, rest_of_weights)

        @block.scalar
        def _(act):
            act.wait_ge(vecs_in.sem, 16)
            act.activation(decay[:], vec[:, 0, :], ACT.Exp).then_inc(decay_exp.sem, 1)
            act.wait_ge(early_const.sem, EARLY_CONST)

            def body(g, f, b, a, n):
                def silus(t, groups):
                    for grp in groups:
                        i = t * NG + grp
                        act.wait_ge(expert_done.sem, expert_done.at(f, i + 1))
                        if combined.rises(f, EPG * (i + 1 - NY)):
                            act.wait_ge(combined.sem, combined.at(f, EPG * (i + 1 - NY)))
                        act.activation(ye[:, i % NY, :], pe[:, i % 2, :], ACT.Silu,
                                       scale=1.0 / WSCALE).then_inc(ye_ready.sem, 1)

                def copy_combined(seq, t):
                    act.wait_ge(t3_done.sem, t3_done.at(seq, t + 1))
                    if on(seq - 1):
                        act.wait_ge(moe_done.sem, moe_done.at(seq - 1))
                    act.copy(combt[:, :, t * P:(t + 1) * P],
                             pt[:, t % 2, 0:C].rearrange("p (h k) -> p h k", h=H)).then_inc(combt_ready.sem, 1)

                def squares(seq, i):
                    act.wait_ge(moe_done.sem, moe_done.at(seq, i + 1))
                    if on(seq - 1):
                        act.wait_ge(rms_ready.sem, rms_ready.at(seq - 1))
                    for t in range(2 * i, 2 * i + 2):
                        if ms_ready.rises(seq, t):
                            act.wait_ge(ms_ready.sem, ms_ready.at(seq, t))
                        act.activation(sq[:], po[:, i, t % 2, :], ACT.Square,
                                       accum_out=ms[:, t:t + 1]).then_inc(ms_ready.sem, 1)

                if on(b) or on(a):
                    act.preload_act_table_set("natural_log_exp_and_others")
                if on(b):
                    act.wait_ge(wkv.sem, wkv.at(b, 6))
                    act.activation(den[:], den[:], ACT.Ln, bias=one[:, 0:1]).then_inc(ln_ready.sem, 1)
                    act.wait_ge(ln_ready.sem, ln_ready.at(b))
                    act.activation(den[:], den[:], ACT.Exp, scale=-1.0).then_inc(rec_ready.sem, 1)
                if on(a):
                    for h in range(H):
                        act.wait_ge(kvr_done.sem, kvr_done.at(a, h + 1))
                        if on(b):
                            act.wait_ge(diffs.sem, diffs.at(b))
                        act.copy(kk[:, h, :], pk[:, h, :]).then_inc(k_ready.sem, 1)
                if on(g):
                    copy_combined(g, 2)
                    copy_combined(g, 3)
                if on(a):
                    for h in range(H):
                        act.wait_ge(kvr_done.sem, kvr_done.at(a, H + h + 1))
                        if on(b):
                            act.wait_ge(wkv.sem, wkv.at(b))
                        act.copy(vv[:, h, :], pk[:, h, :]).then_inc(v_ready.sem, 1)
                if on(g):
                    squares(g, 1)
                if on(a):
                    act.wait_ge(diffs.sem, diffs.at(a, 1))
                    for h in range(H):
                        act.activation(fd[:, h, :], fd[:, h, :], ACT.Exp, bias=decay[:, h:h + 1]).then_inc(e1_ready.sem, 1)
                    act.wait_ge(diffs.sem, diffs.at(a, 2))
                    act.activation(gd[:], gd[:], ACT.Exp).then_inc(e2_ready.sem, 1)
                    act.wait_ge(diffs.sem, diffs.at(a, 3))
                    for h in range(H):
                        act.activation(sd[:, h, :], sd[:, h, :], ACT.Sigmoid, bias=neg_first[:, h:h + 1],
                                       scale=-1.0).then_inc(sg_ready.sem, 1)
                    for h in range(H):
                        act.wait_ge(kvr_done.sem, kvr_done.at(a, 2 * H + h + 1))
                        if on(b):
                            act.wait_ge(wkv.sem, wkv.at(b))
                        act.activation(tr[:, h, :], pk[:, h, :], ACT.Tanh, scale=0.5).then_inc(tr_ready.sem, 1)
                if on(g):
                    for h in range(H):
                        act.wait_ge(t4_done.sem, t4_done.at(g, h + 1))
                        if on(g - 1):
                            act.wait_ge(down_done.sem, down_done.at(g - 1))
                        act.copy(ht[:, h, :], pt[:, h, :]).then_inc(ht_ready.sem, 1)
                if on(f):
                    for h in range(H):
                        act.wait_ge(pw_done.sem, pw_done.at(f, h + 1))
                        if on(g):
                            act.wait_ge(x1l_ready.sem, x1l_ready.at(g))
                        act.activation(x1[:, h, :], pk[:, h, :], ACT.Silu, bias=vec[:, 9, h:h + 1]).then_inc(s1_ready.sem, 1)
                    for h in range(H):
                        act.wait_ge(x1_ready.sem, x1_ready.at(f, h + 1))
                        if on(g):
                            act.wait_ge(moe_done.sem, moe_done.at(g))
                        act.copy(x1h[:, h, :], x1[:, h, :]).then_inc(x1h_ready.sem, 1)
                if on(g):
                    act.wait_ge(down_done.sem, down_done.at(g))
                    if on(g - 1):
                        act.wait_ge(up_done.sem, up_done.at(g - 1))
                    act.activation(ffg[:], pt[0:HID, 0, :], ACT.Gelu, bias=bdown[:, 0:1]).then_inc(ffg_ready.sem, 1)
                if on(f):
                    act.wait_ge(x2_ready.sem, x2_ready.at(f))
                    if on(g):
                        act.wait_ge(xh_ready.sem, xh_ready.at(g))
                    act.copy(x2t[:], x2[:]).then_inc(x2t_ready.sem, 1)
                    silus(0, (0, 1))
                    act.wait_ge(route.sem, route.at(f, 1))
                    if on(g):
                        act.wait_ge(route.sem, route.at(g))
                    act.activation(th[:], gap[:], ACT.Tanh, scale=0.5 / WSCALE).then_inc(tanh_ready.sem, 1)
                    silus(0, (2, 3))
                if on(n):
                    for h in range(H):
                        act.wait_ge(t1_done.sem, t1_done.at(n, h + 1))
                        if on(a):
                            act.wait_ge(mixed.sem, mixed.at(a))
                        act.copy(xt1[:, h, 1:1 + T], pt[:, h, :]).then_inc(xt1_ready.sem, 1)
                if on(f):
                    silus(1, range(NG))
                    copy_combined(f, 0)
                    silus(2, range(NG))
                    copy_combined(f, 1)
                    squares(f, 0)
                if on(b):
                    for h in range(H):
                        act.wait_ge(t2_done.sem, t2_done.at(b, h + 1))
                        if on(f):
                            act.wait_ge(x1_ready.sem, x1_ready.at(f, h + 1))
                        act.copy(xt2[:, h, 2:2 + T], pt[:, h, :]).then_inc(xt2_ready.sem, 1)
                    for h in range(H):
                        act.wait_ge(xt2_ready.sem, xt2_ready.at(b, h + 1))
                        if on(f):
                            act.wait_ge(pw_done.sem, pw_done.at(f))
                        act.activation(cv[:, h, :], xt2[:, h, 2:2 + T], ACT.Identity, bias=vec[:, 8, h:h + 1],
                                       scale=vec[:, 7, h:h + 1]).then_inc(tap_ready.sem, 1)
                if on(f):
                    silus(3, range(NG))

            def rest_of_weights():
                act.wait_ge(small_w_in.sem, small_w_in.per)
                act.wait_ge(dve_const.sem, DVE_CONST)

            schedule(act, body, rest_of_weights)

        @block.vector
        def _(dve):
            v = nc.vector
            dve.wait_ge(vecs_in.sem, 16)
            v.tensor_scalar(neg_first[:], vec[:, 1, :], -1.0, None, ALU.mult).then_inc(early_const.sem, 1)
            v.memset(one[:], 1.0).then_inc(early_const.sem, 1)
            for h in range(H):
                v.memset(xt1[:, h, 0:1], 0.0)
                v.memset(xt2[:, h, 0:2], 0.0)
                v.memset(pp[:, h, 0:1], NEG_INF)
                v.memset(aa[:, h, 0:1], 0.0)
                ins = v.memset(bb[:, h, 0:1], 0.0)
            ins.then_inc(early_const.sem, 1)
            dve.wait_ge(decay_exp.sem, 1)
            v.tensor_scalar(decay[:], decay[:], -1.0, None, ALU.mult).then_inc(early_const.sem, 1)

            def rest_of_constants():
                for h in range(H):
                    dve.wait_ge(stage_in.sem, 16 * (h + 1))
                    v.tensor_scalar(weh[:, h, :], wstage, WSCALE, None, ALU.mult).then_inc(dve_const.sem, 1)
                    dve.wait_ge(dve_const.sem, 2 * h + 1)
                    v.scalar_tensor_tensor(out=wel[:, h, :], in0=wstage, scalar=WSCALE, in1=weh[:, h, :],
                                           op0=ALU.mult, op1=ALU.subtract).then_inc(dve_const.sem, 1)
                done = 2 * H
                dve.wait_ge(small_w_in.sem, small_w_in.per)
                dve.wait_ge(attn_w_in.sem, 16)
                v.tensor_scalar(wrh[:], wrout[:], WSCALE, None, ALU.mult).then_inc(dve_const.sem, 1)
                v.memset(row_is[:], 0.0).then_inc(dve_const.sem, 1)
                dve.wait_ge(dve_const.sem, done + 2)
                v.scalar_tensor_tensor(out=wrl[:], in0=wrout[:], scalar=WSCALE, in1=wrh[:], op0=ALU.mult,
                                       op1=ALU.subtract).then_inc(dve_const.sem, 1)
                v.tensor_scalar(wo2[:], wa[:, 3], 0.5, None, ALU.mult).then_inc(dve_const.sem, 1)
                v.memset(row_is[:, 1:2], 1.0).then_inc(dve_const.sem, 1)
                dve.wait_ge(dve_const.sem, done + 5)
                v.memset(row_is[0:1, 0:1], 1.0).then_inc(dve_const.sem, 1)
                v.memset(row_is[0:1, 1:2], 0.0).then_inc(dve_const.sem, 1)
                v.tensor_scalar(rows[:, 0:OB], rows[:, 0:OB], WSCALE, None, ALU.mult).then_inc(dve_const.sem, 1)
                dve.wait_ge(dve_const.sem, done + 8)
                v.tensor_copy(brow[:], rows[:]).then_inc(dve_const.sem, 1)
                dve.wait_ge(dve_const.sem, done + 9)
                v.tensor_tensor(rows_l[:], rows[:], brow[:], ALU.subtract).then_inc(dve_const.sem, 1)
                dve.wait_ge(dve_const.sem, done + 10)
                v.tensor_scalar(rows_l[:], rows_l[:], row_is[:, 1:2], None, ALU.mult).then_inc(dve_const.sem, 1)
                dve.wait_ge(dve_const.sem, done + 11)
                v.scalar_tensor_tensor(out=brow[:], in0=brow[:], scalar=row_is[:, 0:1], in1=rows_l[:],
                                       op0=ALU.mult, op1=ALU.add).then_inc(dve_const.sem, 1)
                v.memset(ones2[:], 1.0).then_inc(dve_const.sem, 1)
                for e in range(NE):
                    ins = v.memset(rank[:, :, e:e + 1], float(NE - e))
                ins.then_inc(dve_const.sem, 1)
                dve.wait_ge(pool_const.sem, 5)
                v.tensor_copy(ident16[:], ident[:]).then_inc(dve_const.sem, 1)
                dve.wait_ge(dve_const.sem, DVE_CONST)

            def moments_of(seq, src, st, mo, stats, moments, ready):
                if on(seq - 1):
                    dve.wait_ge(ready.sem, ready.at(seq - 1))
                for t in range(NT):
                    v.bn_stats(st[:, t, :], src[:, t, :]).then_inc(stats.sem, 1)
                dve.wait_ge(stats.sem, stats.at(seq))
                v.tensor_tensor(mo[:, 1], st[:, :, 1], st[:, :, 4], ALU.subtract).then_inc(moments.sem, 1)
                v.tensor_tensor(mo[:, 3], st[:, :, 2], st[:, :, 5], ALU.add).then_inc(moments.sem, 1)
                v.tensor_tensor(mo[:, 0], st[:, :, 1], st[:, :, 4], ALU.add).then_inc(moments.sem, 1)
                dve.wait_ge(moments.sem, moments.at(seq, 1))
                v.scalar_tensor_tensor(out=mo[:, 2], in0=mo[:, 1], scalar=C / 4.0, in1=mo[:, 1], op0=ALU.mult,
                                       op1=ALU.mult).then_inc(moments.sem, 1)
                dve.wait_ge(moments.sem, moments.at(seq, 3))
                v.tensor_scalar(mo[:, 0], mo[:, 0], 0.5, None, ALU.mult).then_inc(moments.sem, 1)
                dve.wait_ge(moments.sem, moments.at(seq, 4))
                v.scalar_tensor_tensor(out=mo[:, 3], in0=mo[:, 3], scalar=C * LN_EPS, in1=mo[:, 2], op0=ALU.add,
                                       op1=ALU.add).then_inc(moments.sem, 1)

            def normalise(seq, src, mo, rs, dst, moments, rstd_ready, ready, turned):
                dve.wait_ge(moments.sem, moments.at(seq))
                dve.wait_ge(rstd_ready.sem, rstd_ready.at(seq))
                if on(seq - 1):
                    dve.wait_ge(turned.sem, turned.at(seq - 1))
                for t in range(NT):
                    v.tensor_scalar(dst[:, t, :], src[:, t, :], mo[:, 0, t:t + 1], rs[:, t:t + 1], ALU.subtract,
                                    ALU.mult).then_inc(ready.sem, 1)

            def body(g, f, b, a, n):
                def wkv_step(i):
                    if i == 0:
                        dve.wait_ge(e2_ready.sem, e2_ready.at(a))
                        dve.wait_ge(v_ready.sem, v_ready.at(a))
                        v.tensor_tensor(ev[:], gd[:], vv[:], ALU.mult).then_inc(wkv.sem, 1)
                    elif i in (1, 2):
                        h = i - 1
                        dve.wait_ge(e1_ready.sem, e1_ready.at(a, h + 1))
                        dve.wait_ge(wkv.sem, wkv.at(a, 1))
                        v.tensor_tensor_scan(aa[:, h, 1:1 + T], fd[:, h, :], ev[:, h, :], 0.0, ALU.mult,
                                             ALU.add).then_inc(wkv.sem, 1)
                    elif i in (3, 4):
                        h = i - 3
                        v.tensor_tensor_scan(bb[:, h, 1:1 + T], fd[:, h, :], gd[:, h, :], 0.0, ALU.mult,
                                             ALU.add).then_inc(wkv.sem, 1)
                    elif i == 5:
                        dve.wait_ge(sg_ready.sem, sg_ready.at(a))
                        dve.wait_ge(wkv.sem, wkv.at(a, 5))
                        if on(b):
                            dve.wait_ge(rwkv_ready.sem, rwkv_ready.at(b))
                        v.scalar_tensor_tensor(out=den[:], in0=bb[:, :, 0:T], scalar=1.0, in1=sd[:],
                                               op0=ALU.subtract, op1=ALU.mult).then_inc(wkv.sem, 1)
                    elif i == 6:
                        v.tensor_tensor(num[:], aa[:, :, 0:T], vv[:], ALU.subtract).then_inc(wkv.sem, 1)
                    elif i == 7:
                        dve.wait_ge(wkv.sem, wkv.at(a, 7))
                        v.tensor_tensor(num[:], num[:], sd[:], ALU.mult).then_inc(wkv.sem, 1)
                    elif i == 8:
                        dve.wait_ge(wkv.sem, wkv.at(a, 8))
                        v.tensor_tensor(num[:], num[:], vv[:], ALU.add).then_inc(wkv.sem, 1)
                    elif i == 9:
                        dve.wait_ge(wkv.sem, wkv.at(a, 9))
                        dve.wait_ge(tr_ready.sem, tr_ready.at(a))
                        v.scalar_tensor_tensor(out=num[:], in0=tr[:], scalar=1.0, in1=num[:], op0=ALU.add,
                                               op1=ALU.mult).then_inc(wkv.sem, 1)

                def residual():
                    dve.wait_ge(xres_in.sem, xres_in.at(b))
                    if on(f):
                        dve.wait_ge(xn2_ready.sem, xn2_ready.at(f))
                        dve.wait_ge(x2t_ready.sem, x2t_ready.at(f))
                    for i in range(2):
                        dve.wait_ge(wo_done.sem, wo_done.at(b, i + 1))
                        t = slice(2 * i, 2 * i + 2)
                        v.tensor_tensor(x2[:, t, :], po[:, i], xres[:, t, :], ALU.add).then_inc(x2_ready.sem, 1)

                def moments_proj():
                    dve.wait_ge(x2_ready.sem, x2_ready.at(b))
                    moments_of(b, x2, st2, mo2, stats2, moments2, xn2_ready)

                def normalise_proj():
                    normalise(b, x2, mo2, rstd2, xn2, moments2, rstd2_ready, xn2_ready, t2_done)

                def convolve():
                    for tap in (1, 2):
                        for h in range(H):
                            dve.wait_ge(tap_ready.sem, tap_ready.at(f, h + 1))
                            if tap == 2:
                                dve.wait_ge(conv.sem, conv.at(f, h + 1))
                            v.scalar_tensor_tensor(out=cv[:, h, :], in0=xt2[:, h, 2 - tap:2 - tap + T],
                                                   scalar=vec[:, 7 - tap, h:h + 1], in1=cv[:, h, :],
                                                   op0=ALU.mult, op1=ALU.add).then_inc(conv.sem, 1)

                def mix_difference():
                    dve.wait_ge(xt1_ready.sem, xt1_ready.at(n))
                    if on(a):
                        dve.wait_ge(mixed.sem, mixed.at(a))
                        dve.wait_ge(kvr_done.sem, kvr_done.at(a))
                    v.tensor_tensor(xd[:], xt1[:, :, 1:1 + T], xt1[:, :, 0:T], ALU.subtract).then_inc(mixed.sem, 1)

                def mix(seq, m, dst):
                    dve.wait_ge(mixed.sem, mixed.at(seq, 1))
                    for h in range(H):
                        v.scalar_tensor_tensor(out=dst[:, h, :], in0=xd[:, h, :], scalar=vec[:, m, h:h + 1],
                                               in1=xt1[:, h, 0:T], op0=ALU.mult, op1=ALU.add).then_inc(mixed.sem, 1)

                def last_sum():
                    dve.wait_ge(xh_ready.sem, xh_ready.at(g))
                    if on(g - 1):
                        dve.wait_ge(stored.sem, stored.at(g - 1))
                    for i in range(2):
                        dve.wait_ge(up_done.sem, up_done.at(g, i + 1))
                        t = slice(2 * i, 2 * i + 2)
                        v.tensor_tensor(yo[:, t, :], po[:, i], xh[:, t, :], ALU.add).then_inc(y_ready.sem, 1)

                def scale_h(i):
                    dve.wait_ge(rms_ready.sem, rms_ready.at(g, 3 * i + 3))
                    if on(g - 1):
                        dve.wait_ge(t4_done.sem, t4_done.at(g - 1))
                        dve.wait_ge(xh_ready.sem, xh_ready.at(g - 1))
                    for t in range(2 * i, 2 * i + 2):
                        v.scalar_tensor_tensor(out=hh[:, t, :], in0=po[:, i, t % 2, :], scalar=rms[:, t:t + 1],
                                               in1=normw[:], op0=ALU.mult, op1=ALU.mult).then_inc(h_ready.sem, 1)

                if on(f):
                    convolve()
                if on(a):
                    mix(a, 4, xr)
                    if on(b):
                        dve.wait_ge(diffs.sem, diffs.at(b))
                    for h in range(H):
                        dve.wait_ge(k_ready.sem, k_ready.at(a, h + 1))
                        v.tensor_tensor_scan(pp[:, h, 1:1 + T], decay[:, h:h + 1].to_broadcast([P, T]), kk[:, h, :],
                                             NEG_INF, ALU.add, ALU.max).then_inc(p_ready.sem, 1)
                    dve.wait_ge(p_ready.sem, p_ready.at(a))
                    if on(b):
                        dve.wait_ge(wkv.sem, wkv.at(b))
                    v.tensor_tensor(fd[:], pp[:, :, 0:T], pp[:, :, 1:1 + T], ALU.subtract).then_inc(diffs.sem, 1)
                    v.tensor_tensor(gd[:], kk[:], pp[:, :, 1:1 + T], ALU.subtract).then_inc(diffs.sem, 1)
                    v.tensor_tensor(sd[:], kk[:], pp[:, :, 0:T], ALU.subtract).then_inc(diffs.sem, 1)
                if on(g):
                    scale_h(0)
                if on(b):
                    dve.wait_ge(rec_ready.sem, rec_ready.at(b))
                    dve.wait_ge(wkv.sem, wkv.at(b))
                    if on(f):
                        dve.wait_ge(wo_done.sem, wo_done.at(f))
                    v.tensor_tensor(rwkv[:], num[:], den[:], ALU.mult).then_inc(rwkv_ready.sem, 1)
                if on(g):
                    scale_h(1)
                    dve.wait_ge(h_ready.sem, h_ready.at(g))
                    dve.wait_ge(x2t_ready.sem, x2t_ready.at(g))
                    if on(g - 1):
                        dve.wait_ge(y_ready.sem, y_ready.at(g - 1))
                    v.tensor_tensor(xh[:], x2t[:], hh[:], ALU.add).then_inc(xh_ready.sem, 1)
                if on(a):
                    wkv_step(0)
                    wkv_step(1)
                if on(n):
                    dve.wait_ge(x_in.sem, x_in.at(n))
                    moments_of(n, xa, st1, mo1, stats1, moments1, xn1_ready)
                if on(f):
                    for h in range(H):
                        dve.wait_ge(s1_ready.sem, s1_ready.at(f, h + 1))
                        v.tensor_tensor(x1[:, h, :], x1[:, h, :], xt2[:, h, 2:2 + T], ALU.add).then_inc(x1_ready.sem, 1)
                    for h in range(H):
                        dve.wait_ge(x1_ready.sem, x1_ready.at(f, h + 1))
                        dve.wait_ge(x1h_ready.sem, x1h_ready.at(f, h + 1))
                        if on(g):
                            dve.wait_ge(moe_done.sem, moe_done.at(g))
                        v.tensor_tensor(x1l[:, h, :], x1[:, h, :], x1h[:, h, :], ALU.subtract).then_inc(x1l_ready.sem, 1)
                if on(n):
                    normalise(n, xa, mo1, rstd1, xn1, moments1, rstd1_ready, xn1_ready, t1_done)
                if on(a):
                    wkv_step(2)
                    wkv_step(3)
                if on(b):
                    residual()
                    moments_proj()
                if on(f):
                    wide = lambda x: x.unsqueeze(2).to_broadcast([P, NT, NE])
                    dve.wait_ge(routed.sem, routed.at(f))
                    if on(g):
                        dve.wait_ge(route.sem, route.at(g))
                    v.tensor_copy(lg[:], pk[:, 0, 0:NT * NE].rearrange("p (t e) -> p t e", e=NE)).then_inc(logits_read.sem, 1)
                    dve.wait_ge(logits_read.sem, logits_read.at(f))
                    for j, src in ((0, lg), (1, lg2)):
                        if j == 1:
                            dve.wait_ge(picks.sem, picks.at(f, 5))
                            v.scalar_tensor_tensor(out=lg2[:], in0=sel[:, 0], scalar=NEG_INF, in1=lg[:], op0=ALU.mult,
                                                   op1=ALU.add).then_inc(picks.sem, 1)
                            dve.wait_ge(picks.sem, picks.at(f, 6))
                        v.tensor_reduce(top[:, j], src[:], AX_X, ALU.max).then_inc(picks.sem, 1)
                        dve.wait_ge(picks.sem, picks.at(f, 6 * j + 1))
                        v.tensor_tensor(hit[:, j], src[:], wide(top[:, j]), ALU.is_equal).then_inc(picks.sem, 1)
                        dve.wait_ge(picks.sem, picks.at(f, 6 * j + 2))
                        v.tensor_tensor(hit[:, j], hit[:, j], rank[:], ALU.mult).then_inc(picks.sem, 1)
                        dve.wait_ge(picks.sem, picks.at(f, 6 * j + 3))
                        v.tensor_reduce(first[:, j], hit[:, j], AX_X, ALU.max).then_inc(picks.sem, 1)
                        dve.wait_ge(picks.sem, picks.at(f, 6 * j + 4))
                        v.tensor_tensor(sel[:, j], rank[:], wide(first[:, j]), ALU.is_equal).then_inc(picks.sem, 1)
                    v.tensor_tensor(gap[:], top[:, 0], top[:, 1], ALU.subtract).then_inc(route.sem, 1)
                    if on(a):
                        wkv_step(4)
                    dve.wait_ge(tanh_ready.sem, tanh_ready.at(f))
                    if on(g):
                        dve.wait_ge(combined.sem, combined.at(g))
                    for j, s in ((0, 0.5), (1, -0.5)):
                        v.tensor_scalar(w12[:, j, :], th[:], s, 0.5, ALU.mult, ALU.add).then_inc(route.sem, 1)
                    dve.wait_ge(picks.sem, picks.at(f))
                    dve.wait_ge(route.sem, route.at(f, 3))
                    v.tensor_tensor(sel[:], sel[:], w12[:].unsqueeze(3).to_broadcast([P, 2, NT, NE]),
                                    ALU.mult).then_inc(route.sem, 1)
                    dve.wait_ge(route.sem, route.at(f, 4))
                    v.tensor_tensor(rw[:], sel[:, 0], sel[:, 1], ALU.add).then_inc(route.sem, 1)
                    dve.wait_ge(route.sem, route.at(f, 5))
                    for t in range(NT):
                        for grp in range(NG):
                            i = t * NG + grp
                            dve.wait_ge(ye_ready.sem, ye_ready.at(f, i + 1))
                            for k in range(EPG):
                                e = grp * EPG + k
                                src = ye[:, i % NY, k * C:(k + 1) * C]
                                if e == 0:
                                    if on(g):
                                        dve.wait_ge(t3_done.sem, t3_done.at(g, t + 1))
                                    v.tensor_scalar(comb[:, t, :], src, rw[:, t, 0:1], None,
                                                    ALU.mult).then_inc(combined.sem, 1)
                                else:
                                    dve.wait_ge(combined.sem, combined.at(f, t * NE + e))
                                    v.scalar_tensor_tensor(out=comb[:, t, :], in0=src, scalar=rw[:, t, e:e + 1],
                                                           in1=comb[:, t, :], op0=ALU.mult,
                                                           op1=ALU.add).then_inc(combined.sem, 1)
                            if on(a) and i in WKV_AT:
                                wkv_step(WKV_AT[i])
                            if on(b) and i == 2:
                                normalise_proj()
                            if on(g) and i == 4:
                                last_sum()
                            if on(n) and i == 6:
                                mix_difference()
                            if on(n) and i == 9:
                                mix(n, 2, xk)
                            if on(n) and i == 12:
                                mix(n, 3, xv)
                else:
                    if on(g):
                        last_sum()
                    if on(n):
                        mix_difference()
                        mix(n, 2, xk)
                        mix(n, 3, xv)
                    if on(a):
                        for i in range(4, 10):
                            wkv_step(i)
                    if on(b):
                        normalise_proj()

            schedule(dve, body, rest_of_constants)


def kernel(**inputs):
    import numpy as np
    import concourse.bacc as bacc
    from concourse.bass_utils import run_bass_kernel_spmd

    g = {k: np.asarray(v) for k, v in inputs.items()}
    C = g["L0_attn_x"].shape[2]
    conv = g["L0_ffn_dw_kernel"]
    vectors = [g["L0_attn_time_decay"], g["L0_attn_time_first"], g["L0_attn_time_mix_k"].reshape(C),
               g["L0_attn_time_mix_v"].reshape(C), g["L0_attn_time_mix_r"].reshape(C), conv[:, 0, 0], conv[:, 0, 1],
               conv[:, 0, 2], g["L0_ffn_dw_bias"], g["L0_ffn_pw_b"]]
    arrays = {
        "in_x": g["L0_attn_x"],
        "in_vecs": np.stack([v.reshape(C // P, P).T for v in vectors], axis=1),
        "in_w_attn": np.stack([g["L0_attn_" + n].T for n in ("Wk", "Wv", "Wr", "Wo")]),
        "in_w_pw": g["L0_ffn_pw_w"].T,
        "in_w_router": g["L0_ffn_router_w"].T,
        "in_w_expert": g["L0_ffn_expert_w"].transpose(2, 0, 1).reshape(C, -1),
        "in_w_out": g["L0_ffn_out_w"].T,
        "in_w_down": g["L0_ffn_ff_down_w"].T,
        "in_w_up": g["L0_ffn_ff_up_w"].T,
        "in_b_rows": np.concatenate([g["L0_ffn_expert_b"].reshape(-1), g["L0_ffn_router_b"], g["L0_ffn_out_b"],
                                     g["L0_ffn_ff_up_b"]])[None, :],
        "in_b_down": g["L0_ffn_ff_down_b"][:, None],
        "in_norm_w": g["L0_ffn_norm_w"][None, :],
    }
    arrays = {k: np.ascontiguousarray(v) for k, v in arrays.items()}
    nc = bacc.Bacc("TRN2", target_bir_lowering=False, num_devices=1)
    args = [nc.dram_tensor(k, v.shape, mybir.dt.from_np(v.dtype), kind="ExternalInput").ap() for k, v in arrays.items()]
    shape = g["L0_attn_x"].shape
    out = nc.dram_tensor("out_y", shape, F32, kind="ExternalOutput").ap()
    build(nc, *args, out)
    r = run_bass_kernel_spmd(nc, [arrays], core_ids=[0])
    return r.results[0]["out_y"]
```

```python
from contextlib import ExitStack

import concourse.bass as bass
from concourse import mybir

F32 = mybir.dt.float32
F16 = mybir.dt.float16
AX_X = mybir.AxisListType.X
ALU = mybir.AluOpType
ACT = mybir.ActivationFunctionType

P = 128
NEG_INF = -1e38
LN_EPS = 1e-5
RMS_EPS = 1e-6
WSCALE = 64.0

VECS = ["time_decay", "time_first", "mix_k", "mix_v", "mix_r", "conv0", "conv1", "conv2", "conv_b", "pw_b"]


class Signal:

    def __init__(self, sem, per):
        self.sem, self.per = sem, per

    def at(self, seq, n=None):
        return self.per * seq + (self.per if n is None else n)

    def rises(self, seq, n):
        value = self.at(seq, n)
        return not isinstance(value, int) or value > 0


def build(nc, x, vecs, w_attn, w_pw, w_router, w_expert, w_out, w_down, w_up, b_rows, b_down, norm_w, out):
    B, T, C = x.shape
    H = C // P
    NT = T // P
    NE = w_router.shape[1]
    HID = w_down.shape[1]
    NG = NE * C // T
    EPG = NE // NG
    RB, UB, OB = NE * C, NE * C + NE, NE * C + NE + C
    NROW = OB + C
    NV = len(VECS)

    with ExitStack() as ctx:
        def sb(name, shape, dt=F32):
            return ctx.enter_context(nc.sbuf_tensor(name, shape, dt))

        def ps(name, shape):
            return ctx.enter_context(nc.psum_tensor(name, shape, F32))

        def sig(name, per):
            return Signal(ctx.enter_context(nc.semaphore(name)), per)

        vec = sb("vec", [P, NV, H])
        decay = sb("decay", [P, H])
        neg_first = sb("neg_first", [P, H])
        keep = sb("keep", [P, 3, H])
        wa = sb("wa", [P, 4, H, C])
        wpw = sb("wpw", [P, H, C])
        wo2 = sb("wo2", [P, H, C])
        wout = sb("wout", [P, H, C])
        wdown = sb("wdown", [P, H, 2 * HID])
        bdown = sb("bdown", [2 * HID, 1])
        wup = sb("wup", [2 * HID, C])
        wuh = sb("wuh", [2 * HID, C], F16)
        wul = sb("wul", [HID + 2, C], F16)
        wrout = sb("wrout", [P, H, NE])
        wrh = sb("wrh", [P, H, NE], F16)
        wrl = sb("wrl", [P, H, NE], F16)
        weh = sb("weh", [P, H, NE * C], F16)
        wel = sb("wel", [P, H, NE * C], F16)
        BP = 8
        bias = sb("bias", [BP, NROW // BP])
        bias_h = sb("bias_h", [BP, NROW // BP], F16)
        bias_l = sb("bias_l", [BP, NROW // BP], F16)
        brow = sb("brow", [2, NROW], F16)
        ones2 = sb("ones2", [2, P], F16)
        one = sb("one", [P, 1])
        normw = sb("normw", [P, C])
        ident = sb("ident", [P, P])
        ident16 = sb("ident16", [P, P], F16)
        rank = sb("rank", [P, NT, NE])
        minus_half = sb("minus_half", [P, NT])
        wscale = sb("wscale", [P, 1])
        sqrt_c = sb("sqrt_c", [P, NT])
        half_sqrt_c = sb("half_sqrt_c", [P, NT])
        ln_eps_c = sb("ln_eps_c", [P, NT])
        quarter_c = sb("quarter_c", [P, NT])
        rms_eps_c = sb("rms_eps_c", [P, NT])

        xa = sb("xa", [P, NT, C])
        st1 = sb("st1", [P, NT, 6])
        mo1 = sb("mo1", [P, 4, NT])
        pw1 = sb("pw1", [P, 2, NT])
        rstd1 = sb("rstd1", [P, NT])
        shift1 = sb("shift1", [P, NT])
        xn1 = sb("xn1", [P, NT, C])
        xt1 = sb("xt1", [P, H, 1 + T])
        xk = sb("xk", [P, H, T])
        xv = sb("xv", [P, H, T])
        xr = sb("xr", [P, H, T])
        kk = sb("kk", [P, H, T])
        vv = sb("vv", [P, H, T])
        pp = sb("pp", [P, H, 1 + T])
        fd = sb("fd", [P, H, T])
        gd = sb("gd", [P, H, T])
        sd = sb("sd", [P, H, T])
        ev = sb("ev", [P, H, T])
        aa = sb("aa", [P, H, 1 + T])
        bb = sb("bb", [P, H, 1 + T])
        num = sb("num", [P, H, T])
        den = sb("den", [P, H, T])
        tr = sb("tr", [P, H, T])
        rwkv = sb("rwkv", [P, H, T])
        xres = sb("xres", [P, NT, C])
        x2 = sb("x2", [P, NT, C])
        x2t = sb("x2t", [P, NT, C])
        st2 = sb("st2", [P, NT, 6])
        mo2 = sb("mo2", [P, 4, NT])
        pw2 = sb("pw2", [P, 2, NT])
        rstd2 = sb("rstd2", [P, NT])
        shift2 = sb("shift2", [P, NT])
        xn2 = sb("xn2", [P, NT, C])
        xt2 = sb("xt2", [P, H, 2 + T])
        cv = sb("cv", [P, H, T])
        x1 = sb("x1", [P, H, T])
        x1h = sb("x1h", [P, H, T], F16)
        x1l = sb("x1l", [P, H, T], F16)
        lg = sb("lg", [P, NT, NE])
        lg2 = sb("lg2", [P, NT, NE])
        hit = sb("hit", [P, 2, NT, NE])
        top = sb("top", [P, 2, NT])
        first = sb("first", [P, 2, NT])
        gap = sb("gap", [P, NT])
        th = sb("th", [P, NT])
        w12 = sb("w12", [P, 2, NT])
        sel = sb("sel", [P, 2, NT, NE])
        rw = sb("rw", [P, NT, NE])
        NY = 8
        ye = sb("ye", [P, NY, T])
        wstage = ye[:].rearrange("p (h y) t -> p h (y t)", h=H)
        comb = sb("comb", [P, NT, C])
        combt = sb("combt", [P, H, T])
        sq = sb("sq", [P, C])
        ms = sb("ms", [P, NT])
        msv = sb("msv", [P, NT])
        msp = sb("msp", [P, NT])
        rms = sb("rms", [P, NT])
        hh = sb("hh", [P, NT, C])
        ht = sb("ht", [P, H, T])
        xh = sb("xh", [P, NT, C])
        ffg = sb("ffg", [2 * HID, T])
        ffs = sb("ffs", [2 * HID, T], F16)
        ffh = sb("ffh", [HID + 2, T], F16)
        yo = sb("yo", [P, NT, C])

        pt = ps("pt", [P, 2, T])
        pk = ps("pk", [P, 2, T])
        pe = ps("pe", [P, 2, T])
        po = ps("po", [P, 2, 2, C])

        vecs_in = sig("vecs_in", 16)
        attn_w_in = sig("attn_w_in", 16)
        small_w_in = sig("small_w_in", 16 * 10)
        bias_in = sig("bias_in", 16 * 2)
        stage_in = sig("stage_in", 16)
        decay_exp = sig("decay_exp", 1)
        pool_const = sig("pool_const", 11)
        early_const = sig("early_const", 1)
        dve_const = sig("dve_const", 1)
        weh_ready = sig("weh_ready", H)
        wel_ready = sig("wel_ready", 2 * H)
        brow_in = sig("brow_in", 16 * 5)
        x_in = sig("x_in", 16)
        stats1 = sig("stats1", NT)
        moments1 = sig("moments1", 7)
        rstd1_ready = sig("rstd1_ready", 4)
        xn1_ready = sig("xn1_ready", NT)
        t1_done = sig("t1_done", 2)
        xt1_ready = sig("xt1_ready", 2)
        faded = [sig("faded_" + m, 2) for m in "kvr"]
        mixed = sig("mixed", 6)
        kvr_done = sig("kvr_done", 6)
        k_ready = sig("k_ready", 2)
        v_ready = sig("v_ready", 2)
        tr_ready = sig("tr_ready", 2)
        p_ready = sig("p_ready", 2)
        diffs = sig("diffs", 3)
        e1_ready = sig("e1_ready", 2)
        e2_ready = sig("e2_ready", 1)
        sg_ready = sig("sg_ready", 2)
        wkv = sig("wkv", 10)
        rwkv_ready = sig("rwkv_ready", 1)
        ln_ready = sig("ln_ready", 1)
        rec_ready = sig("rec_ready", 1)
        wo_done = sig("wo_done", 2)
        xres_in = sig("xres_in", 16)
        x2_ready = sig("x2_ready", 2)
        stats2 = sig("stats2", NT)
        moments2 = sig("moments2", 7)
        rstd2_ready = sig("rstd2_ready", 4)
        xn2_ready = sig("xn2_ready", NT)
        t2_done = sig("t2_done", 2)
        xt2_ready = sig("xt2_ready", 2)
        tap_ready = sig("tap_ready", 2)
        conv = sig("conv", 4)
        pw_done = sig("pw_done", 2)
        s1_ready = sig("s1_ready", 2)
        x1_ready = sig("x1_ready", 2)
        x1h_ready = sig("x1h_ready", 2)
        x1l_ready = sig("x1l_ready", 2)
        routed = sig("routed", 1)
        logits_read = sig("logits_read", 1)
        picks = sig("picks", 11)
        route = sig("route", 5)
        tanh_ready = sig("tanh_ready", 1)
        expert_done = sig("expert_done", NT * NG)
        ye_ready = sig("ye_ready", NT * NG)
        combined = sig("combined", NT * NE)
        t3_done = sig("t3_done", NT)
        combt_ready = sig("combt_ready", NT)
        moe_done = sig("moe_done", 2)
        ms_ready = sig("ms_ready", NT)
        rms_ready = sig("rms_ready", 6)
        h_ready = sig("h_ready", NT)
        xh_ready = sig("xh_ready", 1)
        x2t_ready = sig("x2t_ready", 1)
        t4_done = sig("t4_done", 2)
        ht_ready = sig("ht_ready", 2)
        down_done = sig("down_done", 1)
        ffg_ready = sig("ffg_ready", 1)
        ffh_ready = sig("ffh_ready", 2)
        ffl_ready = sig("ffl_ready", 1)
        up_done = sig("up_done", 2)
        y_ready = sig("y_ready", 2)
        stored = sig("stored", 16)

        x_tok = x.rearrange("b (t p) c -> b p t c", p=P)
        out_tok = out.rearrange("b (t p) c -> b p t c", p=P)
        WKV_AT = {3: 5, 5: 6, 7: 7, 8: 8, 10: 9}
        EARLY_CONST = 5
        BIAS_CONST = 6
        DVE_CONST = BIAS_CONST + 4

        def on(seq):
            return not isinstance(seq, int) or 0 <= seq < B

        def dram_seq(ap, seq):
            return ap[bass.ds(seq, 1)].rearrange("a p t c -> p (a t) c")

        def schedule(eng, body, between={}):
            for g in range(-4, 1):
                body(g, g + 1, g + 2, g + 3, g + 4)
                if g in between:
                    between[g]()
            with eng.Fori(1, B - 5) as g:
                body(g, g + 1, g + 2, g + 3, g + 4)
            for g in range(B - 5, B):
                body(g, g + 1, g + 2, g + 3, g + 4)

        block = ctx.enter_context(nc.Block())

        @block.sync
        def _(sp):
            halves = lambda w: w.rearrange("(h p) c -> p h c", p=P)
            sp.dma_start(xa[:], dram_seq(x_tok, 0)).then_inc(x_in.sem, 16)
            sp.dma_start(vec[:], vecs).then_inc(vecs_in.sem, 16)
            sp.dma_start(wa[:], w_attn.rearrange("m (h p) c -> p m h c", p=P)).then_inc(attn_w_in.sem, 16)
            sp.dma_start(wpw[:], halves(w_pw)).then_inc(small_w_in.sem, 16)
            sp.dma_start(wrout[:], halves(w_router)).then_inc(small_w_in.sem, 16)
            sp.dma_start(wout[:], halves(w_out)).then_inc(small_w_in.sem, 16)
            for part in (slice(0, HID), slice(HID, 2 * HID)):
                sp.dma_start(wdown[:, :, part], halves(w_down)).then_inc(small_w_in.sem, 16)
                sp.dma_start(wup[part, :], w_up).then_inc(small_w_in.sem, 16)
                sp.dma_start(bdown[part, :], b_down).then_inc(small_w_in.sem, 16)
            sp.dma_start(normw[:], norm_w.to_broadcast([P, C])).then_inc(small_w_in.sem, 16)
            spread = lambda cols: cols.rearrange("a (p k) -> (a p) k", p=BP)
            sp.dma_start(bias[:, 0:OB // BP], spread(b_rows[:, 0:OB])).then_inc(bias_in.sem, 16)
            sp.dma_start(bias[:, OB // BP:], spread(b_rows[:, OB:])).then_inc(bias_in.sem, 16)

            def body(g, f, b, a, n):
                if on(n + 1):
                    if on(n):
                        sp.wait_ge(xn1_ready.sem, xn1_ready.at(n))
                    sp.dma_start(xa[:], dram_seq(x_tok, n + 1)).then_inc(x_in.sem, 16)
                if on(a):
                    if on(b):
                        sp.wait_ge(x2_ready.sem, x2_ready.at(b))
                    sp.dma_start(xres[:], dram_seq(x_tok, a)).then_inc(xres_in.sem, 16)
                if on(g):
                    sp.wait_ge(y_ready.sem, y_ready.at(g))
                    sp.dma_start(dram_seq(out_tok, g), yo[:]).then_inc(stored.sem, 16)

            def stage_experts():
                for h in range(H):
                    sp.dma_start(wstage[:, h], w_expert[h * P:(h + 1) * P, :]).then_inc(stage_in.sem, 16)

            def gather_biases():
                sp.wait_ge(dve_const.sem, BIAS_CONST)
                for row, part in ((0, bias_h), (1, bias_l)):
                    for c0, c1 in ((0, OB), (OB, NROW)):
                        sp.dma_start(brow[row:row + 1, c0:c1].rearrange("a (p k) -> a p k", p=BP),
                                     part[:, c0 // BP:c1 // BP]).then_inc(brow_in.sem, 16)
                sp.wait_ge(brow_in.sem, 16 * 4)
                sp.dma_start(wul[HID:HID + 2, :], brow[:, UB:UB + C]).then_inc(brow_in.sem, 16)

            schedule(sp, body, {-4: stage_experts, -3: gather_biases})
            sp.wait_ge(stored.sem, stored.at(B - 1))

        @block.gpsimd
        def _(pool):
            nc.gpsimd.memset(ident[:], 0.0).then_inc(pool_const.sem, 1)
            pool.wait_ge(pool_const.sem, 1)
            nc.gpsimd.affine_select(out=ident[:], in_=ident[:], compare_op=ALU.not_equal, fill=1.0, base=0,
                                    pattern=[[-1, P]], channel_multiplier=1).then_inc(pool_const.sem, 1)
            nc.gpsimd.memset(minus_half[:], -0.5).then_inc(pool_const.sem, 1)
            nc.gpsimd.memset(sqrt_c[:], float(C) ** 0.5).then_inc(pool_const.sem, 1)
            nc.gpsimd.memset(half_sqrt_c[:], -0.5 * float(C) ** 0.5).then_inc(pool_const.sem, 1)
            nc.gpsimd.memset(ln_eps_c[:], LN_EPS * C).then_inc(pool_const.sem, 1)
            nc.gpsimd.memset(quarter_c[:], C / 4.0).then_inc(pool_const.sem, 1)
            nc.gpsimd.memset(rms_eps_c[:], RMS_EPS * C).then_inc(pool_const.sem, 1)
            nc.gpsimd.memset(ones2[:], 1.0).then_inc(pool_const.sem, 1)
            nc.gpsimd.memset(wscale[:], WSCALE).then_inc(pool_const.sem, 1)
            for e in range(NE):
                ins = nc.gpsimd.memset(rank[:, :, e:e + 1], float(NE - e))
            ins.then_inc(pool_const.sem, 1)
            pool.wait_ge(pool_const.sem, pool_const.per)

            def rstd(seq, st, mo, pw, dst, shift, stats, moments, ready, used):
                pool.wait_ge(stats.sem, stats.at(seq))
                if on(seq - 1):
                    pool.wait_ge(ready.sem, ready.at(seq - 1))
                    pool.wait_ge(used.sem, used.at(seq - 1))
                nc.gpsimd.tensor_tensor(mo[:, 1], st[:, :, 1], st[:, :, 4], ALU.subtract).then_inc(moments.sem, 1)
                nc.gpsimd.tensor_tensor(mo[:, 3], st[:, :, 2], st[:, :, 5], ALU.add).then_inc(moments.sem, 1)
                nc.gpsimd.tensor_tensor(mo[:, 0], st[:, :, 1], st[:, :, 4], ALU.add).then_inc(moments.sem, 1)
                pool.wait_ge(moments.sem, moments.at(seq, 1))
                nc.gpsimd.tensor_tensor(mo[:, 2], mo[:, 1], mo[:, 1], ALU.mult).then_inc(moments.sem, 1)
                pool.wait_ge(moments.sem, moments.at(seq, 2))
                nc.gpsimd.tensor_tensor(mo[:, 3], mo[:, 3], ln_eps_c[:], ALU.add).then_inc(moments.sem, 1)
                pool.wait_ge(moments.sem, moments.at(seq, 4))
                nc.gpsimd.tensor_tensor(mo[:, 2], mo[:, 2], quarter_c[:], ALU.mult).then_inc(moments.sem, 1)
                pool.wait_ge(moments.sem, moments.at(seq, 6))
                nc.gpsimd.tensor_tensor(mo[:, 3], mo[:, 3], mo[:, 2], ALU.add).then_inc(moments.sem, 1)
                pool.wait_ge(moments.sem, moments.at(seq))
                nc.gpsimd.tensor_tensor(pw[:, 0], mo[:, 3], minus_half[:], ALU.pow).then_inc(ready.sem, 1)
                pool.wait_ge(ready.sem, ready.at(seq, 1))
                nc.gpsimd.tensor_tensor(dst[:], pw[:, 0], sqrt_c[:], ALU.mult).then_inc(ready.sem, 1)
                nc.gpsimd.tensor_tensor(pw[:, 1], pw[:, 0], half_sqrt_c[:], ALU.mult).then_inc(ready.sem, 1)
                pool.wait_ge(ready.sem, ready.at(seq, 3))
                nc.gpsimd.tensor_tensor(shift[:], mo[:, 0], pw[:, 1], ALU.mult).then_inc(ready.sem, 1)

            def inverse_rms(seq, i):
                t = slice(2 * i, 2 * i + 2)
                pool.wait_ge(ms_ready.sem, ms_ready.at(seq, 2 * i + 2))
                if on(seq - 1):
                    pool.wait_ge(rms_ready.sem, rms_ready.at(seq - 1))
                    pool.wait_ge(h_ready.sem, h_ready.at(seq - 1))
                nc.gpsimd.tensor_tensor(msv[:, t], ms[:, t], rms_eps_c[:, t], ALU.add).then_inc(rms_ready.sem, 1)
                pool.wait_ge(rms_ready.sem, rms_ready.at(seq, 3 * i + 1))
                nc.gpsimd.tensor_tensor(msp[:, t], msv[:, t], minus_half[:, t], ALU.pow).then_inc(rms_ready.sem, 1)
                pool.wait_ge(rms_ready.sem, rms_ready.at(seq, 3 * i + 2))
                nc.gpsimd.tensor_tensor(rms[:, t], msp[:, t], sqrt_c[:, t], ALU.mult).then_inc(rms_ready.sem, 1)

            def body(g, f, b, a, n):
                if on(g):
                    inverse_rms(g, 1)
                if on(n):
                    rstd(n, st1, mo1, pw1, rstd1, shift1, stats1, moments1, rstd1_ready, xn1_ready)
                if on(b):
                    rstd(b, st2, mo2, pw2, rstd2, shift2, stats2, moments2, rstd2_ready, xn2_ready)
                if on(f):
                    inverse_rms(f, 0)

            def expert_low_parts():
                for h in range(H):
                    pool.wait_ge(weh_ready.sem, h + 1)
                    nc.gpsimd.tensor_tensor(wstage[:, h], wstage[:, h], wscale[:].to_broadcast([P, NE * C]),
                                            ALU.mult).then_inc(wel_ready.sem, 1)
                    pool.wait_ge(wel_ready.sem, 2 * h + 1)
                    nc.gpsimd.tensor_tensor(wel[:, h, :], wstage[:, h], weh[:, h, :],
                                            ALU.subtract).then_inc(wel_ready.sem, 1)

            schedule(pool, body, {-3: expert_low_parts})

        @block.tensor
        def _(te):
            def transpose_all(src, done):
                for h in range(H):
                    for t in range(NT):
                        mm = nc.tensor.transpose(pt[:, h, t * P:(t + 1) * P], src[:, t, h * P:(h + 1) * P], ident[:])
                    mm.then_inc(done.sem, 1)

            def product(dst, weight, m, src, done):
                for h in range(H):
                    mm = nc.tensor.matmul(dst, weight[:, h, m * P:(m + 1) * P], src[:, h, :],
                                          start=h == 0, stop=h == H - 1)
                mm.then_inc(done.sem, 1)

            def body(g, f, b, a, n):
                draining = on(f) and not on(a)

                def experts(t, groups=range(NG)):
                    tok = slice(t * P, (t + 1) * P)
                    for grp in groups:
                        i = t * NG + grp
                        if ye_ready.rises(f, i - 1):
                            te.wait_ge(ye_ready.sem, ye_ready.at(f, i - 1))
                        dst, cols = pe[:, i % 2, :], slice(grp * T, (grp + 1) * T)
                        nc.tensor.matmul(dst, ones2[:], brow[:, cols], start=True, stop=False)
                        for h in range(H):
                            nc.tensor.matmul(dst, x1h[:, h, tok], weh[:, h, cols], start=False, stop=False)
                            nc.tensor.matmul(dst, x1h[:, h, tok], wel[:, h, cols], start=False, stop=False)
                            mm = nc.tensor.matmul(dst, x1l[:, h, tok], weh[:, h, cols], start=False, stop=h == H - 1)
                        mm.then_inc(expert_done.sem, 1)

                def turn_combined(seq, t):
                    te.wait_ge(combined.sem, combined.at(seq, NE * (t + 1)))
                    if t < 2:
                        if on(n):
                            te.wait_ge(xt1_ready.sem, xt1_ready.at(n, t + 1))
                        if on(g):
                            te.wait_ge(ffg_ready.sem, ffg_ready.at(g))
                        if t == 1 and on(b):
                            te.wait_ge(xt2_ready.sem, xt2_ready.at(b, 2))
                    else:
                        te.wait_ge(combt_ready.sem, combt_ready.at(seq, t - 1))
                        if on(seq + 1):
                            te.wait_ge(xt2_ready.sem, xt2_ready.at(seq + 1, t - 1))
                    for h in range(H):
                        mm = nc.tensor.transpose(pt[:, t % 2, h * P:(h + 1) * P], comb[:, t, h * P:(h + 1) * P],
                                                 ident[:])
                    mm.then_inc(t3_done.sem, 1)

                def mix_out(seq, i):
                    if on(seq + 1):
                        te.wait_ge(x2_ready.sem, x2_ready.at(seq + 1, i + 1))
                    if on(seq - 1):
                        te.wait_ge(y_ready.sem, y_ready.at(seq - 1, i + 1))
                    for t in range(2 * i, 2 * i + 2):
                        tok = slice(t * P, (t + 1) * P)
                        te.wait_ge(combt_ready.sem, combt_ready.at(seq, t + 1))
                        dst = po[:, i, t % 2, :]
                        nc.tensor.matmul(dst, ones2[:], brow[:, OB:OB + C], start=True, stop=False)
                        for h in range(H):
                            part = dst[:, h * P:(h + 1) * P]
                            nc.tensor.matmul(part, x1h[:, h, tok], ident16[:], start=False, stop=False)
                            nc.tensor.matmul(part, x1l[:, h, tok], ident16[:], start=False, stop=False)
                        for h in range(H):
                            mm = nc.tensor.matmul(dst, combt[:, h, tok], wout[:, h, :], start=False, stop=h == H - 1)
                    mm.then_inc(moe_done.sem, 1)

                def turn_front():
                    te.wait_ge(xn1_ready.sem, xn1_ready.at(n))
                    if on(g):
                        te.wait_ge(ffg_ready.sem, ffg_ready.at(g))
                    if on(a):
                        te.wait_ge(xt1_ready.sem, xt1_ready.at(a))
                    if on(f):
                        te.wait_ge(xt2_ready.sem, xt2_ready.at(f))
                    transpose_all(xn1, t1_done)

                def project():
                    te.wait_ge(rwkv_ready.sem, rwkv_ready.at(b))
                    for i in range(2):
                        if on(g):
                            te.wait_ge(h_ready.sem, h_ready.at(g, 2 * i + 2))
                        if on(f):
                            te.wait_ge(x2_ready.sem, x2_ready.at(f, i + 1))
                        for t in range(2 * i, 2 * i + 2):
                            for h in range(H):
                                mm = nc.tensor.matmul(po[:, i, t % 2, :], rwkv[:, h, t * P:(t + 1) * P], wo2[:, h, :],
                                                      start=h == 0, stop=h == H - 1)
                        mm.then_inc(wo_done.sem, 1)

                def turn_proj():
                    te.wait_ge(xn2_ready.sem, xn2_ready.at(b))
                    if on(f):
                        te.wait_ge(combt_ready.sem, combt_ready.at(f, 1))
                    if on(n):
                        te.wait_ge(xt1_ready.sem, xt1_ready.at(n))
                    transpose_all(xn2, t2_done)

                def pointwise(half):
                    te.wait_ge(conv.sem, conv.at(f))
                    if on(a):
                        te.wait_ge(tr_ready.sem, tr_ready.at(a, half + 1))
                    else:
                        te.wait_ge(logits_read.sem, logits_read.at(g))
                        if on(b):
                            te.wait_ge(tr_ready.sem, tr_ready.at(b, half + 1))
                    product(pk[:, half, :], wpw, half, cv, pw_done)

                def feed_up():
                    te.wait_ge(ffh_ready.sem, ffh_ready.at(g))
                    te.wait_ge(ffl_ready.sem, ffl_ready.at(g))
                    for i in range(2):
                        if on(b):
                            te.wait_ge(x2_ready.sem, x2_ready.at(b, i + 1))
                        for t in range(2 * i, 2 * i + 2):
                            dst = po[:, i, t % 2, :]
                            nc.tensor.matmul(dst, ffs[:, t * P:(t + 1) * P], wuh[:], start=True, stop=False)
                            mm = nc.tensor.matmul(dst, ffh[:, t * P:(t + 1) * P], wul[:], start=False, stop=True)
                        mm.then_inc(up_done.sem, 1)

                if on(a):
                    te.wait_ge(mixed.sem, mixed.at(a, 2))
                    for half in range(H):
                        if on(b):
                            te.wait_ge(tr_ready.sem, tr_ready.at(b, half + 1))
                        if on(g):
                            te.wait_ge(s1_ready.sem, s1_ready.at(g, half + 1))
                            te.wait_ge(logits_read.sem, logits_read.at(g))
                        product(pk[:, half, :], wa[:, 0], half, xk, kvr_done)
                if draining:
                    pointwise(0)
                if on(g):
                    turn_combined(g, 2)
                if on(a):
                    te.wait_ge(mixed.sem, mixed.at(a, 4))
                    for half in range(H):
                        te.wait_ge(k_ready.sem, k_ready.at(a, half + 1))
                        product(pk[:, half, :], wa[:, 1], half, xv, kvr_done)
                if on(g):
                    turn_combined(g, 3)
                    mix_out(g, 1)
                if draining:
                    pointwise(1)
                if on(b) and not on(f):
                    project()
                if on(a):
                    te.wait_ge(mixed.sem, mixed.at(a))
                    for half in range(H):
                        te.wait_ge(v_ready.sem, v_ready.at(a, half + 1))
                        product(pk[:, half, :], wa[:, 2], half, xr, kvr_done)
                if on(g):
                    te.wait_ge(h_ready.sem, h_ready.at(g))
                    te.wait_ge(combt_ready.sem, combt_ready.at(g))
                    if on(f):
                        te.wait_ge(xt2_ready.sem, xt2_ready.at(f))
                    if on(a):
                        te.wait_ge(xt1_ready.sem, xt1_ready.at(a))
                    transpose_all(hh, t4_done)
                if on(f) and not draining:
                    pointwise(0)
                    pointwise(1)
                if on(g):
                    te.wait_ge(ht_ready.sem, ht_ready.at(g))
                    for h in range(H):
                        mm = nc.tensor.matmul(pt[:, 0, :], wdown[:, h, :], ht[:, h, :], start=h == 0,
                                              stop=h == H - 1)
                    mm.then_inc(down_done.sem, 1)
                if on(b) and on(f):
                    project()
                if on(f):
                    te.wait_ge(x1h_ready.sem, x1h_ready.at(f))
                    te.wait_ge(x1l_ready.sem, x1l_ready.at(f))
                    te.wait_ge(s1_ready.sem, s1_ready.at(f, 1))
                    for t in range(NT):
                        tok = slice(t * P, (t + 1) * P)
                        dst = pk[:, 0, t * NE:(t + 1) * NE]
                        nc.tensor.matmul(dst, ones2[:], brow[:, RB:RB + NE], start=True, stop=False)
                        for h in range(H):
                            nc.tensor.matmul(dst, x1h[:, h, tok], wrh[:, h, :], start=False, stop=False)
                            nc.tensor.matmul(dst, x1h[:, h, tok], wrl[:, h, :], start=False, stop=False)
                            mm = nc.tensor.matmul(dst, x1l[:, h, tok], wrh[:, h, :], start=False, stop=h == H - 1)
                    mm.then_inc(routed.sem, 1)
                    experts(0)
                if on(g):
                    feed_up()
                if on(f):
                    experts(1, (0, 1, 2))
                if on(n):
                    turn_front()
                if on(f):
                    experts(1, (3,))
                    turn_combined(f, 0)
                    experts(2)
                    experts(3, (0, 1))
                if on(b):
                    turn_proj()
                if on(f):
                    experts(3, (2,))
                    turn_combined(f, 1)
                    mix_out(f, 0)
                    experts(3, (3,))

            def for_attention():
                te.wait_ge(attn_w_in.sem, 16)

            def for_projection():
                te.wait_ge(dve_const.sem, 1)

            def for_experts():
                te.wait_ge(small_w_in.sem, small_w_in.per)
                te.wait_ge(dve_const.sem, DVE_CONST)
                te.wait_ge(weh_ready.sem, weh_ready.per)
                te.wait_ge(wel_ready.sem, wel_ready.per)
                te.wait_ge(brow_in.sem, brow_in.per)

            te.wait_ge(pool_const.sem, pool_const.per)
            te.wait_ge(early_const.sem, EARLY_CONST)
            schedule(te, body, {-4: for_attention, -3: for_projection, -2: for_experts})

        @block.scalar
        def _(act):
            act.wait_ge(vecs_in.sem, 16)
            act.activation(decay[:], vec[:, 0, :], ACT.Exp).then_inc(decay_exp.sem, 1)
            act.wait_ge(early_const.sem, EARLY_CONST)

            def body(g, f, b, a, n):
                draining = on(f) and not on(a)

                def fade(m, h):
                    act.wait_ge(xt1_ready.sem, xt1_ready.at(n, h + 1))
                    if on(a):
                        act.wait_ge(kvr_done.sem, kvr_done.at(a, H * (m + 1)))
                    act.activation((xk, xv, xr)[m][:, h, :], xt1[:, h, 0:T], ACT.Identity,
                                   scale=keep[:, m, h:h + 1]).then_inc(faded[m].sem, 1)

                def pointwise_silu(h):
                    act.wait_ge(pw_done.sem, pw_done.at(f, h + 1))
                    if on(g):
                        act.wait_ge(x1l_ready.sem, x1l_ready.at(g))
                    act.activation(x1[:, h, :], pk[:, h, :], ACT.Silu, bias=vec[:, 9, h:h + 1]).then_inc(s1_ready.sem, 1)

                def normalise(seq, src, rs, shift, dst, rstd_ready, ready, turned, tiles):
                    act.wait_ge(rstd_ready.sem, rstd_ready.at(seq))
                    if on(seq - 1):
                        act.wait_ge(turned.sem, turned.at(seq - 1))
                    for t in tiles:
                        act.activation(dst[:, t, :], src[:, t, :], ACT.Identity, scale=rs[:, t:t + 1],
                                       bias=shift[:, t:t + 1]).then_inc(ready.sem, 1)

                def normalise_front(tiles):
                    normalise(n, xa, rstd1, shift1, xn1, rstd1_ready, xn1_ready, t1_done, tiles)

                def normalise_proj(tiles):
                    normalise(b, x2, rstd2, shift2, xn2, rstd2_ready, xn2_ready, t2_done, tiles)

                def silus(t, groups):
                    for grp in groups:
                        i = t * NG + grp
                        act.wait_ge(expert_done.sem, expert_done.at(f, i + 1))
                        if combined.rises(f, EPG * (i + 1 - NY)):
                            act.wait_ge(combined.sem, combined.at(f, EPG * (i + 1 - NY)))
                        act.activation(ye[:, i % NY, :], pe[:, i % 2, :], ACT.Silu,
                                       scale=1.0 / WSCALE).then_inc(ye_ready.sem, 1)

                def copy_combined(seq, t):
                    act.wait_ge(t3_done.sem, t3_done.at(seq, t + 1))
                    if on(seq - 1):
                        act.wait_ge(moe_done.sem, moe_done.at(seq - 1))
                    act.copy(combt[:, :, t * P:(t + 1) * P],
                             pt[:, t % 2, 0:C].rearrange("p (h k) -> p h k", h=H)).then_inc(combt_ready.sem, 1)

                def squares(seq, i):
                    act.wait_ge(moe_done.sem, moe_done.at(seq, i + 1))
                    if on(seq - 1):
                        act.wait_ge(rms_ready.sem, rms_ready.at(seq - 1))
                    for t in range(2 * i, 2 * i + 2):
                        if ms_ready.rises(seq, t):
                            act.wait_ge(ms_ready.sem, ms_ready.at(seq, t))
                        act.activation(sq[:], po[:, i, t % 2, :], ACT.Square,
                                       accum_out=ms[:, t:t + 1]).then_inc(ms_ready.sem, 1)

                if on(b) or on(a):
                    act.preload_act_table_set("natural_log_exp_and_others")
                if on(a):
                    for h in range(H):
                        act.wait_ge(kvr_done.sem, kvr_done.at(a, h + 1))
                        if on(b):
                            act.wait_ge(diffs.sem, diffs.at(b))
                        act.copy(kk[:, h, :], pk[:, h, :]).then_inc(k_ready.sem, 1)
                if on(g):
                    copy_combined(g, 2)
                if on(b):
                    act.wait_ge(wkv.sem, wkv.at(b, 6))
                    act.activation(den[:], den[:], ACT.Ln, bias=one[:, 0:1]).then_inc(ln_ready.sem, 1)
                    act.wait_ge(ln_ready.sem, ln_ready.at(b))
                    act.activation(den[:], den[:], ACT.Exp, scale=-1.0).then_inc(rec_ready.sem, 1)
                if draining:
                    act.preload_act_table_set("silu_and_others")
                    pointwise_silu(0)
                if on(a):
                    for h in range(H):
                        act.wait_ge(kvr_done.sem, kvr_done.at(a, H + h + 1))
                        if on(b):
                            act.wait_ge(wkv.sem, wkv.at(b))
                        act.copy(vv[:, h, :], pk[:, h, :]).then_inc(v_ready.sem, 1)
                if on(g):
                    copy_combined(g, 3)
                if on(a):
                    act.wait_ge(diffs.sem, diffs.at(a, 1))
                    for h in range(H):
                        act.activation(fd[:, h, :], fd[:, h, :], ACT.Exp, bias=decay[:, h:h + 1]).then_inc(e1_ready.sem, 1)
                    act.wait_ge(diffs.sem, diffs.at(a, 2))
                    act.activation(gd[:], gd[:], ACT.Exp).then_inc(e2_ready.sem, 1)
                if on(g):
                    squares(g, 1)
                if draining:
                    pointwise_silu(1)
                if on(n) and on(a) and not on(b):
                    normalise_front(range(NT))
                if on(a):
                    act.preload_act_table_set("sigmoid_and_others")
                    for h in range(H):
                        act.wait_ge(kvr_done.sem, kvr_done.at(a, 2 * H + h + 1))
                        if on(b):
                            act.wait_ge(wkv.sem, wkv.at(b))
                        act.activation(tr[:, h, :], pk[:, h, :], ACT.Tanh, scale=0.5).then_inc(tr_ready.sem, 1)
                if on(g):
                    for h in range(H):
                        act.wait_ge(t4_done.sem, t4_done.at(g, h + 1))
                        if on(g - 1):
                            act.wait_ge(down_done.sem, down_done.at(g - 1))
                        act.copy(ht[:, h, :], pt[:, h, :]).then_inc(ht_ready.sem, 1)
                if on(a):
                    act.wait_ge(diffs.sem, diffs.at(a, 3))
                    for h in range(H):
                        act.activation(sd[:, h, :], sd[:, h, :], ACT.Sigmoid, bias=neg_first[:, h:h + 1],
                                       scale=-1.0).then_inc(sg_ready.sem, 1)
                if on(f) and not draining:
                    act.preload_act_table_set("silu_and_others")
                if on(f):
                    if not draining:
                        pointwise_silu(0)
                        pointwise_silu(1)
                    for h in range(H):
                        act.wait_ge(x1_ready.sem, x1_ready.at(f, h + 1))
                        if on(g):
                            act.wait_ge(moe_done.sem, moe_done.at(g))
                        act.copy(x1h[:, h, :], x1[:, h, :]).then_inc(x1h_ready.sem, 1)
                if on(g):
                    act.preload_act_table_set("gelu_and_others")
                    act.wait_ge(down_done.sem, down_done.at(g))
                    if on(g - 1):
                        act.wait_ge(ffl_ready.sem, ffl_ready.at(g - 1))
                        act.wait_ge(up_done.sem, up_done.at(g - 1))
                    act.activation(ffg[:], pt[:, 0, :], ACT.Gelu, bias=bdown[:, 0:1]).then_inc(ffg_ready.sem, 1)
                    act.wait_ge(ffg_ready.sem, ffg_ready.at(g))
                    act.copy(ffs[:], ffg[:]).then_inc(ffh_ready.sem, 1)
                    act.copy(ffh[0:HID, :], ffg[0:HID, :]).then_inc(ffh_ready.sem, 1)
                if on(f):
                    act.wait_ge(x2_ready.sem, x2_ready.at(f))
                    if on(g):
                        act.wait_ge(xh_ready.sem, xh_ready.at(g))
                    act.copy(x2t[:], x2[:]).then_inc(x2t_ready.sem, 1)
                    act.preload_act_table_set("silu_and_others")
                    silus(0, (0, 1))
                    act.wait_ge(route.sem, route.at(f, 1))
                    if on(g):
                        act.wait_ge(route.sem, route.at(g))
                    act.activation(th[:], gap[:], ACT.Tanh, scale=0.5 / WSCALE).then_inc(tanh_ready.sem, 1)
                    for i in range(2, 6):
                        silus(i // NG, (i % NG,))
                        if on(n):
                            normalise_front((i - 2,))
                    silus(1, (2,))
                if on(n) and not on(f) and (on(b) or not on(a)):
                    normalise_front(range(NT))
                if on(n):
                    for h in range(H):
                        act.wait_ge(t1_done.sem, t1_done.at(n, h + 1))
                        if on(a):
                            act.wait_ge(mixed.sem, mixed.at(a))
                        act.copy(xt1[:, h, 1:1 + T], pt[:, h, :]).then_inc(xt1_ready.sem, 1)
                    if not on(f):
                        for m in range(3):
                            for h in range(H):
                                fade(m, h)
                if on(b) and not on(f):
                    normalise_proj(range(NT))
                if on(f):
                    silus(1, (3,))
                    if on(n):
                        fade(0, 0)
                    copy_combined(f, 0)
                    silus(2, (0,))
                    if on(n):
                        fade(0, 1)
                    for i in range(1, NG + 1):
                        silus(2 + i // NG, (i % NG,))
                        if on(b):
                            normalise_proj((i - 1,))
                    silus(3, (1,))
                if on(b):
                    for h in range(H):
                        act.wait_ge(t2_done.sem, t2_done.at(b, h + 1))
                        if on(f):
                            act.wait_ge(x1_ready.sem, x1_ready.at(f, h + 1))
                        act.copy(xt2[:, h, 2:2 + T], pt[:, h, :]).then_inc(xt2_ready.sem, 1)
                if on(f):
                    if on(n):
                        fade(2, 0)
                    silus(3, (2,))
                    copy_combined(f, 1)
                if on(b):
                    for h in range(H):
                        act.wait_ge(xt2_ready.sem, xt2_ready.at(b, h + 1))
                        if on(f):
                            act.wait_ge(pw_done.sem, pw_done.at(f))
                        act.activation(cv[:, h, :], xt2[:, h, 2:2 + T], ACT.Identity, bias=vec[:, 8, h:h + 1],
                                       scale=vec[:, 7, h:h + 1]).then_inc(tap_ready.sem, 1)
                if on(f):
                    if on(n):
                        fade(1, 0)
                        fade(1, 1)
                        fade(2, 1)
                    silus(3, (3,))
                    squares(f, 0)

            def expert_weights():
                act.wait_ge(small_w_in.sem, small_w_in.per)
                for h in range(H):
                    act.wait_ge(stage_in.sem, 16 * H)
                    act.activation(weh[:, h, :], wstage[:, h], ACT.Copy, scale=WSCALE).then_inc(weh_ready.sem, 1)

            def for_experts():
                act.wait_ge(wel_ready.sem, wel_ready.per)

            schedule(act, body, {-3: expert_weights, -2: for_experts})

        @block.vector
        def _(dve):
            v = nc.vector
            dve.wait_ge(vecs_in.sem, 16)
            v.tensor_scalar(neg_first[:], vec[:, 1, :], -1.0, None, ALU.mult).then_inc(early_const.sem, 1)
            v.memset(one[:], 1.0).then_inc(early_const.sem, 1)
            v.tensor_scalar(keep[:], vec[:, 2:5, :], -1.0, 1.0, ALU.mult, ALU.add).then_inc(early_const.sem, 1)
            for h in range(H):
                v.memset(xt1[:, h, 0:1], 0.0)
                v.memset(xt2[:, h, 0:2], 0.0)
                v.memset(pp[:, h, 0:1], NEG_INF)
                v.memset(aa[:, h, 0:1], 0.0)
                ins = v.memset(bb[:, h, 0:1], 0.0)
            ins.then_inc(early_const.sem, 1)
            dve.wait_ge(decay_exp.sem, 1)
            v.tensor_scalar(decay[:], decay[:], -1.0, None, ALU.mult).then_inc(early_const.sem, 1)

            def attention_constants():
                dve.wait_ge(attn_w_in.sem, 16)
                v.tensor_scalar(wo2[:], wa[:, 3], 0.5, None, ALU.mult).then_inc(dve_const.sem, 1)
                dve.wait_ge(bias_in.sem, bias_in.per)
                v.tensor_scalar(bias[:, 0:OB // BP], bias[:, 0:OB // BP], WSCALE, None, ALU.mult).then_inc(dve_const.sem, 1)
                dve.wait_ge(small_w_in.sem, small_w_in.per)
                v.tensor_scalar(wrh[:], wrout[:], WSCALE, None, ALU.mult).then_inc(dve_const.sem, 1)
                dve.wait_ge(dve_const.sem, 2)
                v.tensor_copy(bias_h[:], bias[:]).then_inc(dve_const.sem, 1)
                dve.wait_ge(dve_const.sem, 3)
                v.scalar_tensor_tensor(out=wrl[:], in0=wrout[:], scalar=WSCALE, in1=wrh[:], op0=ALU.mult,
                                       op1=ALU.subtract).then_inc(dve_const.sem, 1)
                dve.wait_ge(dve_const.sem, 4)
                v.tensor_tensor(bias_l[:], bias[:], bias_h[:], ALU.subtract).then_inc(dve_const.sem, 1)

            def rest_of_constants():
                dve.wait_ge(pool_const.sem, pool_const.per)
                v.tensor_copy(ident16[:], ident[:]).then_inc(dve_const.sem, 1)
                v.tensor_scalar(wuh[:], wup[:], WSCALE, None, ALU.mult).then_inc(dve_const.sem, 1)
                dve.wait_ge(dve_const.sem, BIAS_CONST + 2)
                v.scalar_tensor_tensor(out=wul[0:HID, :], in0=wup[0:HID, :], scalar=WSCALE, in1=wuh[0:HID, :],
                                       op0=ALU.mult, op1=ALU.subtract).then_inc(dve_const.sem, 1)
                v.memset(ffh[HID:, :], 1.0).then_inc(dve_const.sem, 1)
                dve.wait_ge(dve_const.sem, DVE_CONST)

            def body(g, f, b, a, n):
                early = not on(f)

                def wkv_step(i):
                    if i == 0:
                        dve.wait_ge(e2_ready.sem, e2_ready.at(a))
                        dve.wait_ge(v_ready.sem, v_ready.at(a))
                        v.tensor_tensor(ev[:], gd[:], vv[:], ALU.mult).then_inc(wkv.sem, 1)
                    elif i in (1, 2):
                        h = i - 1
                        dve.wait_ge(e1_ready.sem, e1_ready.at(a, h + 1))
                        dve.wait_ge(wkv.sem, wkv.at(a, 1))
                        v.tensor_tensor_scan(aa[:, h, 1:1 + T], fd[:, h, :], ev[:, h, :], 0.0, ALU.mult,
                                             ALU.add).then_inc(wkv.sem, 1)
                    elif i in (3, 4):
                        h = i - 3
                        v.tensor_tensor_scan(bb[:, h, 1:1 + T], fd[:, h, :], gd[:, h, :], 0.0, ALU.mult,
                                             ALU.add).then_inc(wkv.sem, 1)
                    elif i == 5:
                        dve.wait_ge(sg_ready.sem, sg_ready.at(a))
                        dve.wait_ge(wkv.sem, wkv.at(a, 5))
                        if on(b):
                            dve.wait_ge(rwkv_ready.sem, rwkv_ready.at(b))
                        v.scalar_tensor_tensor(out=den[:], in0=bb[:, :, 0:T], scalar=1.0, in1=sd[:],
                                               op0=ALU.subtract, op1=ALU.mult).then_inc(wkv.sem, 1)
                    elif i == 6:
                        v.tensor_tensor(num[:], aa[:, :, 0:T], vv[:], ALU.subtract).then_inc(wkv.sem, 1)
                    elif i == 7:
                        dve.wait_ge(wkv.sem, wkv.at(a, 7))
                        v.tensor_tensor(num[:], num[:], sd[:], ALU.mult).then_inc(wkv.sem, 1)
                    elif i == 8:
                        dve.wait_ge(wkv.sem, wkv.at(a, 8))
                        v.tensor_tensor(num[:], num[:], vv[:], ALU.add).then_inc(wkv.sem, 1)
                    elif i == 9:
                        dve.wait_ge(wkv.sem, wkv.at(a, 9))
                        dve.wait_ge(tr_ready.sem, tr_ready.at(a))
                        v.scalar_tensor_tensor(out=num[:], in0=tr[:], scalar=1.0, in1=num[:], op0=ALU.add,
                                               op1=ALU.mult).then_inc(wkv.sem, 1)

                def residual(i):
                    dve.wait_ge(xres_in.sem, xres_in.at(b))
                    if on(f):
                        dve.wait_ge(xn2_ready.sem, xn2_ready.at(f))
                        dve.wait_ge(x2t_ready.sem, x2t_ready.at(f))
                    dve.wait_ge(wo_done.sem, wo_done.at(b, i + 1))
                    t = slice(2 * i, 2 * i + 2)
                    v.tensor_tensor(x2[:, t, :], po[:, i], xres[:, t, :], ALU.add).then_inc(x2_ready.sem, 1)

                def stats_proj():
                    dve.wait_ge(x2_ready.sem, x2_ready.at(b))
                    if on(f):
                        dve.wait_ge(rstd2_ready.sem, rstd2_ready.at(f))
                    for t in range(NT):
                        v.bn_stats(st2[:, t, :], x2[:, t, :]).then_inc(stats2.sem, 1)

                def convolve(seq):
                    for tap in (1, 2):
                        for h in range(H):
                            dve.wait_ge(tap_ready.sem, tap_ready.at(seq, h + 1))
                            if tap == 2:
                                dve.wait_ge(conv.sem, conv.at(seq, h + 1))
                            v.scalar_tensor_tensor(out=cv[:, h, :], in0=xt2[:, h, 2 - tap:2 - tap + T],
                                                   scalar=vec[:, 7 - tap, h:h + 1], in1=cv[:, h, :],
                                                   op0=ALU.mult, op1=ALU.add).then_inc(conv.sem, 1)

                def mix(seq, m, dst):
                    for h in range(H):
                        dve.wait_ge(faded[m].sem, faded[m].at(seq, h + 1))
                        v.scalar_tensor_tensor(out=dst[:, h, :], in0=xt1[:, h, 1:1 + T], scalar=vec[:, 2 + m, h:h + 1],
                                               in1=dst[:, h, :], op0=ALU.mult, op1=ALU.add).then_inc(mixed.sem, 1)

                def last_sum():
                    dve.wait_ge(xh_ready.sem, xh_ready.at(g))
                    if on(g - 1):
                        dve.wait_ge(stored.sem, stored.at(g - 1))
                    for i in range(2):
                        dve.wait_ge(up_done.sem, up_done.at(g, i + 1))
                        t = slice(2 * i, 2 * i + 2)
                        v.scalar_tensor_tensor(out=yo[:, t, :], in0=po[:, i], scalar=1.0 / WSCALE, in1=xh[:, t, :],
                                               op0=ALU.mult, op1=ALU.add).then_inc(y_ready.sem, 1)

                def stats_front():
                    dve.wait_ge(x_in.sem, x_in.at(n))
                    if on(a):
                        dve.wait_ge(rstd1_ready.sem, rstd1_ready.at(a))
                    for t in range(NT):
                        v.bn_stats(st1[:, t, :], xa[:, t, :]).then_inc(stats1.sem, 1)

                def quotient():
                    dve.wait_ge(rec_ready.sem, rec_ready.at(b))
                    dve.wait_ge(wkv.sem, wkv.at(b))
                    if on(f):
                        dve.wait_ge(wo_done.sem, wo_done.at(f))
                    v.tensor_tensor(rwkv[:], num[:], den[:], ALU.mult).then_inc(rwkv_ready.sem, 1)

                def scale_h(i):
                    dve.wait_ge(rms_ready.sem, rms_ready.at(g, 3 * i + 3))
                    if on(g - 1):
                        dve.wait_ge(t4_done.sem, t4_done.at(g - 1))
                        dve.wait_ge(xh_ready.sem, xh_ready.at(g - 1))
                    for t in range(2 * i, 2 * i + 2):
                        v.scalar_tensor_tensor(out=hh[:, t, :], in0=po[:, i, t % 2, :], scalar=rms[:, t:t + 1],
                                               in1=normw[:], op0=ALU.mult, op1=ALU.mult).then_inc(h_ready.sem, 1)

                if on(b) and early:
                    quotient()
                if on(n) and early:
                    stats_front()
                if on(a):
                    if on(b):
                        dve.wait_ge(diffs.sem, diffs.at(b))
                    for h in range(H):
                        dve.wait_ge(k_ready.sem, k_ready.at(a, h + 1))
                        v.tensor_tensor_scan(pp[:, h, 1:1 + T], decay[:, h:h + 1].to_broadcast([P, T]), kk[:, h, :],
                                             NEG_INF, ALU.add, ALU.max).then_inc(p_ready.sem, 1)
                    dve.wait_ge(p_ready.sem, p_ready.at(a))
                    if on(b):
                        dve.wait_ge(wkv.sem, wkv.at(b))
                    v.tensor_tensor(fd[:], pp[:, :, 0:T], pp[:, :, 1:1 + T], ALU.subtract).then_inc(diffs.sem, 1)
                    v.tensor_tensor(gd[:], kk[:], pp[:, :, 1:1 + T], ALU.subtract).then_inc(diffs.sem, 1)
                    mix(a, 2, xr)
                if on(g):
                    scale_h(0)
                if on(f) and on(a):
                    convolve(f)
                if on(g):
                    scale_h(1)
                if on(a):
                    v.tensor_tensor(sd[:], kk[:], pp[:, :, 0:T], ALU.subtract).then_inc(diffs.sem, 1)
                if on(b) and not early:
                    quotient()
                if on(g):
                    dve.wait_ge(h_ready.sem, h_ready.at(g))
                    dve.wait_ge(x2t_ready.sem, x2t_ready.at(g))
                    if on(g - 1):
                        dve.wait_ge(y_ready.sem, y_ready.at(g - 1))
                    v.tensor_tensor(xh[:], x2t[:], hh[:], ALU.add).then_inc(xh_ready.sem, 1)
                if on(a):
                    wkv_step(0)
                    wkv_step(1)
                if on(f):
                    for h in range(H):
                        dve.wait_ge(s1_ready.sem, s1_ready.at(f, h + 1))
                        v.tensor_tensor(x1[:, h, :], x1[:, h, :], xt2[:, h, 2:2 + T], ALU.add).then_inc(x1_ready.sem, 1)
                    for h in range(H):
                        dve.wait_ge(x1_ready.sem, x1_ready.at(f, h + 1))
                        dve.wait_ge(x1h_ready.sem, x1h_ready.at(f, h + 1))
                        if on(g):
                            dve.wait_ge(moe_done.sem, moe_done.at(g))
                        v.tensor_tensor(x1l[:, h, :], x1[:, h, :], x1h[:, h, :], ALU.subtract).then_inc(x1l_ready.sem, 1)
                if on(n) and not early:
                    stats_front()
                if on(f):
                    wide = lambda x: x.unsqueeze(2).to_broadcast([P, NT, NE])

                    def largest(j, src):
                        v.tensor_reduce(top[:, j], src[:], AX_X, ALU.max).then_inc(picks.sem, 1)

                    def ranked(j, src):
                        dve.wait_ge(picks.sem, picks.at(f, 6 * j + 1))
                        v.tensor_tensor(hit[:, j], src[:], wide(top[:, j]), ALU.is_equal).then_inc(picks.sem, 1)
                        dve.wait_ge(picks.sem, picks.at(f, 6 * j + 2))
                        v.tensor_tensor(hit[:, j], hit[:, j], rank[:], ALU.mult).then_inc(picks.sem, 1)

                    def first_of(j):
                        dve.wait_ge(picks.sem, picks.at(f, 6 * j + 3))
                        v.tensor_reduce(first[:, j], hit[:, j], AX_X, ALU.max).then_inc(picks.sem, 1)

                    def select(j):
                        dve.wait_ge(picks.sem, picks.at(f, 6 * j + 4))
                        v.tensor_tensor(sel[:, j], rank[:], wide(first[:, j]), ALU.is_equal).then_inc(picks.sem, 1)

                    dve.wait_ge(routed.sem, routed.at(f))
                    if on(g):
                        dve.wait_ge(route.sem, route.at(g))
                    v.tensor_copy(lg[:], pk[:, 0, 0:NT * NE].rearrange("p (t e) -> p t e", e=NE)).then_inc(logits_read.sem, 1)
                if on(a):
                    wkv_step(2)
                if on(f):
                    dve.wait_ge(logits_read.sem, logits_read.at(f))
                    largest(0, lg)
                if on(a):
                    wkv_step(3)
                if on(f):
                    ranked(0, lg)
                if on(g):
                    dve.wait_ge(ffh_ready.sem, ffh_ready.at(g, 1))
                    v.tensor_tensor(ffs[HID:], ffg[HID:], ffs[HID:], ALU.subtract).then_inc(ffl_ready.sem, 1)
                if on(f):
                    first_of(0)
                if on(b):
                    residual(0)
                if on(f):
                    select(0)
                if on(b):
                    residual(1)
                if on(f):
                    dve.wait_ge(picks.sem, picks.at(f, 5))
                    v.scalar_tensor_tensor(out=lg2[:], in0=sel[:, 0], scalar=NEG_INF, in1=lg[:], op0=ALU.mult,
                                           op1=ALU.add).then_inc(picks.sem, 1)
                if on(a):
                    wkv_step(4)
                if on(f):
                    dve.wait_ge(picks.sem, picks.at(f, 6))
                    largest(1, lg2)
                    dve.wait_ge(picks.sem, picks.at(f, 7))
                    v.tensor_tensor(gap[:], top[:, 0], top[:, 1], ALU.subtract).then_inc(route.sem, 1)
                    ranked(1, lg2)
                    first_of(1)
                    select(1)
                if on(b) and not on(f):
                    stats_proj()
                if on(f):
                    dve.wait_ge(tanh_ready.sem, tanh_ready.at(f))
                    if on(g):
                        dve.wait_ge(combined.sem, combined.at(g))
                    for j, s in ((0, 0.5), (1, -0.5)):
                        v.tensor_scalar(w12[:, j, :], th[:], s, 0.5, ALU.mult, ALU.add).then_inc(route.sem, 1)
                    dve.wait_ge(picks.sem, picks.at(f))
                    dve.wait_ge(route.sem, route.at(f, 3))
                    v.tensor_tensor(sel[:], sel[:], w12[:].unsqueeze(3).to_broadcast([P, 2, NT, NE]),
                                    ALU.mult).then_inc(route.sem, 1)
                    dve.wait_ge(route.sem, route.at(f, 4))
                    v.tensor_tensor(rw[:], sel[:, 0], sel[:, 1], ALU.add).then_inc(route.sem, 1)
                    dve.wait_ge(route.sem, route.at(f, 5))
                    for t in range(NT):
                        for grp in range(NG):
                            i = t * NG + grp
                            dve.wait_ge(ye_ready.sem, ye_ready.at(f, i + 1))
                            for k in range(EPG):
                                e = grp * EPG + k
                                src = ye[:, i % NY, k * C:(k + 1) * C]
                                if e == 0:
                                    if on(g):
                                        dve.wait_ge(t3_done.sem, t3_done.at(g, t + 1))
                                    v.tensor_scalar(comb[:, t, :], src, rw[:, t, 0:1], None,
                                                    ALU.mult).then_inc(combined.sem, 1)
                                else:
                                    dve.wait_ge(combined.sem, combined.at(f, t * NE + e))
                                    v.scalar_tensor_tensor(out=comb[:, t, :], in0=src, scalar=rw[:, t, e:e + 1],
                                                           in1=comb[:, t, :], op0=ALU.mult,
                                                           op1=ALU.add).then_inc(combined.sem, 1)
                            if on(a) and i in WKV_AT:
                                wkv_step(WKV_AT[i])
                            if on(b) and i == 1:
                                stats_proj()
                            if on(b) and not on(n) and i == 14:
                                convolve(b)
                            if on(g) and i == 4:
                                last_sum()
                            if on(n) and i == 12:
                                mix(n, 0, xk)
                            if on(n) and i == 14:
                                mix(n, 1, xv)
                else:
                    if on(g):
                        last_sum()
                    if on(n):
                        mix(n, 0, xk)
                        mix(n, 1, xv)
                    if on(a):
                        for i in range(5, 10):
                            wkv_step(i)

            schedule(dve, body, {-4: attention_constants, -3: rest_of_constants})


def kernel(**inputs):
    import numpy as np
    import concourse.bacc as bacc
    from concourse.bass_utils import run_bass_kernel_spmd

    g = {k: np.asarray(v) for k, v in inputs.items()}
    C = g["L0_attn_x"].shape[2]
    conv = g["L0_ffn_dw_kernel"]
    vectors = [g["L0_attn_time_decay"], g["L0_attn_time_first"], g["L0_attn_time_mix_k"].reshape(C),
               g["L0_attn_time_mix_v"].reshape(C), g["L0_attn_time_mix_r"].reshape(C), conv[:, 0, 0], conv[:, 0, 1],
               conv[:, 0, 2], g["L0_ffn_dw_bias"], g["L0_ffn_pw_b"]]
    arrays = {
        "in_x": g["L0_attn_x"],
        "in_vecs": np.stack([v.reshape(C // P, P).T for v in vectors], axis=1),
        "in_w_attn": np.stack([g["L0_attn_" + n].T for n in ("Wk", "Wv", "Wr", "Wo")]),
        "in_w_pw": g["L0_ffn_pw_w"].T,
        "in_w_router": g["L0_ffn_router_w"].T,
        "in_w_expert": g["L0_ffn_expert_w"].transpose(2, 0, 1).reshape(C, -1),
        "in_w_out": g["L0_ffn_out_w"].T,
        "in_w_down": g["L0_ffn_ff_down_w"].T,
        "in_w_up": g["L0_ffn_ff_up_w"].T,
        "in_b_rows": np.concatenate([g["L0_ffn_expert_b"].reshape(-1), g["L0_ffn_router_b"],
                                     g["L0_ffn_ff_up_b"], g["L0_ffn_out_b"]])[None, :],
        "in_b_down": g["L0_ffn_ff_down_b"][:, None],
        "in_norm_w": g["L0_ffn_norm_w"][None, :],
    }
    arrays = {k: np.ascontiguousarray(v) for k, v in arrays.items()}
    nc = bacc.Bacc("TRN2", target_bir_lowering=False, num_devices=1)
    args = [nc.dram_tensor(k, v.shape, mybir.dt.from_np(v.dtype), kind="ExternalInput").ap() for k, v in arrays.items()]
    shape = g["L0_attn_x"].shape
    out = nc.dram_tensor("out_y", shape, F32, kind="ExternalOutput").ap()
    build(nc, *args, out)
    r = run_bass_kernel_spmd(nc, [arrays], core_ids=[0])
    return r.results[0]["out_y"]
```
